# Optimizing a Trainium2 kernel written in Bass

```python
import numpy as np
import jax
import jax.numpy as jnp

def _softmax(x, axis=-1):
    return jax.nn.softmax(x, axis=axis)

def _gelu(x):
    return jax.nn.gelu(x, approximate=True)

def _silu(x):
    return jax.nn.silu(x)

def _sigmoid(x):
    return jax.nn.sigmoid(x)

def _layernorm(x, axis=-1, eps=1e-05):
    m = jnp.mean(x, axis=axis, keepdims=True)
    v = jnp.var(x, axis=axis, keepdims=True)
    return (x - m) / jnp.sqrt(v + eps)

def _scatter_add(tgt, idx, src, axis=0):
    return tgt.at[idx].add(src)

def _segment_sum(src, seg, n):
    return jax.ops.segment_sum(src, seg, n)
kernel_name = 'mk_cond_resid_d4_seqx_r4_54a409'

def setup_inputs(seed: int=0):
    np.random.seed(seed)
    _w = jnp.asarray

    def _rec_inputs():
        import jax
        import jax.numpy as jnp
        _rk = jax.random.key(seed)
        x = -0.000125 + 0.9999 * jax.random.normal(jax.random.fold_in(_rk, 1), (32, 64, 1024), jnp.float32)
        _lenS = 64 - jax.random.randint(jax.random.fold_in(_rk, 7), (32,), 0, max(1, 64 // 4) + 1, jnp.int32)
        _lenS2 = 64 - jax.random.randint(jax.random.fold_in(_rk, 8), (32,), 0, max(1, 64 // 4) + 1, jnp.int32)
        itok_B_1_7 = jax.random.randint(jax.random.fold_in(_rk, 11), (32,), 1, 8, jnp.int32)
        itok_B_6_15 = jax.random.randint(jax.random.fold_in(_rk, 12), (32,), 6, 16, jnp.int32)
        itok_B_3_7 = jax.random.randint(jax.random.fold_in(_rk, 13), (32,), 3, 8, jnp.int32)
        itok_B_0_15 = jax.random.randint(jax.random.fold_in(_rk, 14), (32,), 0, 16, jnp.int32)
        return (x, itok_B_1_7, itok_B_6_15, itok_B_3_7, itok_B_0_15)
    x, itok_B_1_7, itok_B_6_15, itok_B_3_7, itok_B_0_15 = _rec_inputs()

    def _L0_cond_setup():
        import jax, jax.numpy as jnp
        import numpy as np
        B, S, D_IN, D_OUT = (4, 512, 1024, 1024)
        N_ADAPTERS, MAX_RANK = (8, 16)
        key = jax.random.key(seed)
        ks = jax.random.split(key, 7)
        x = jax.random.normal(ks[0], (B, S, D_IN), dtype=jnp.float32)
        weight = jax.random.normal(ks[1], (D_OUT, D_IN), dtype=jnp.float32) * (1.0 / np.sqrt(D_IN))
        bias = jax.random.normal(ks[2], (D_OUT,), dtype=jnp.float32) * 0.01
        lora_a_weights = jax.random.normal(ks[3], (N_ADAPTERS, MAX_RANK, D_IN), dtype=jnp.float32) * (1.0 / np.sqrt(D_IN))
        lora_b_weights = jax.random.normal(ks[4], (N_ADAPTERS, D_OUT, MAX_RANK), dtype=jnp.float32) * 0.02
        scaling_factors = jax.random.uniform(ks[5], (N_ADAPTERS,), dtype=jnp.float32, minval=0.5, maxval=2.0)
        adapter_id = jax.random.randint(ks[6], (B,), 0, N_ADAPTERS, dtype=jnp.int64)
        return {'x': x, 'weight': weight, 'bias': bias, 'lora_a_weights': lora_a_weights, 'lora_b_weights': lora_b_weights, 'scaling_factors': scaling_factors, 'adapter_id': adapter_id}
    _L0_cond_all = _L0_cond_setup()
    _L0_cond_in = {k: v for k, v in _L0_cond_all.items() if k in ('weight', 'bias', 'lora_a_weights', 'lora_b_weights', 'scaling_factors')}
    del _L0_cond_all

    def _L1_cond_setup():
        import jax, jax.numpy as jnp
        import numpy as np
        B, S, D_IN, D_OUT = (4, 512, 1024, 1024)
        RANK, MAX_LORAS = (16, 32)
        key = jax.random.key(seed)
        ks = jax.random.split(key, 6)
        x = jax.random.normal(ks[0], (B, S, D_IN), dtype=jnp.float32)
        adapter_ids = jax.random.randint(ks[1], (B,), 0, MAX_LORAS)
        base_weight = jax.random.normal(ks[2], (D_OUT, D_IN), dtype=jnp.float32) * D_IN ** (-0.5)
        base_bias = jax.random.normal(ks[3], (D_OUT,), dtype=jnp.float32) * 0.01
        lora_A_w = jax.random.normal(ks[4], (MAX_LORAS, RANK, D_IN), dtype=jnp.float32) * D_IN ** (-0.5)
        lora_B_w = jax.random.normal(ks[5], (MAX_LORAS, D_OUT, RANK), dtype=jnp.float32) * RANK ** (-0.5)
        return {'x': x, 'adapter_ids': adapter_ids, 'base_weight': base_weight, 'base_bias': base_bias, 'lora_A_w': lora_A_w, 'lora_B_w': lora_B_w}
    _L1_cond_all = _L1_cond_setup()
    _L1_cond_in = {k: v for k, v in _L1_cond_all.items() if k in ('base_weight', 'base_bias', 'lora_A_w', 'lora_B_w')}
    del _L1_cond_all

    def _L2_cond_setup():
        import jax, jax.numpy as jnp
        import numpy as np
        MAX_LORAS, OUT, IN = (8, 1024, 1024)
        B, S = (4, 512)
        key = jax.random.key(seed)
        k1, k2, k3 = jax.random.split(key, 3)
        x = jax.random.normal(k1, (B, S, IN), dtype=jnp.float32)
        weight = jax.random.normal(k2, (MAX_LORAS, OUT, IN), dtype=jnp.float32) * 0.02
        adapter_ids = jax.random.randint(k3, (B,), 0, MAX_LORAS, dtype=jnp.int32)
        return {'x': x, 'weight': weight, 'adapter_ids': adapter_ids}
    _L2_cond_all = _L2_cond_setup()
    _L2_cond_in = {k: v for k, v in _L2_cond_all.items() if k in ('weight',)}
    del _L2_cond_all

    def _L3_cond_setup():
        import jax, jax.numpy as jnp
        import numpy as np
        NUM_CONDITIONS = 16
        IN_CH = 64
        OUT_CH = 64
        B = 64
        T = 1024
        key = jax.random.key(seed)
        k_x, k_w, k_c = jax.random.split(key, 3)
        x = jax.random.normal(k_x, (B, IN_CH, T), dtype=jnp.float32)
        bound = float(np.sqrt(6.0 / IN_CH))
        weights = jax.random.uniform(k_w, (NUM_CONDITIONS, IN_CH, OUT_CH), dtype=jnp.float32, minval=-bound, maxval=bound)
        condition = jax.random.randint(k_c, (B,), 0, NUM_CONDITIONS, dtype=jnp.int64)
        return {'x': x, 'weights': weights, 'condition': condition}
    _L3_cond_all = _L3_cond_setup()
    _L3_cond_in = {k: v for k, v in _L3_cond_all.items() if k in ('weights',)}
    del _L3_cond_all
    return {'x': x, 'itok_B_1_7': itok_B_1_7, 'itok_B_6_15': itok_B_6_15, 'itok_B_3_7': itok_B_3_7, 'itok_B_0_15': itok_B_0_15, 'L0_cond_weight': _L0_cond_in['weight'], 'L0_cond_bias': _L0_cond_in['bias'], 'L0_cond_lora_a_weights': _L0_cond_in['lora_a_weights'], 'L0_cond_lora_b_weights': _L0_cond_in['lora_b_weights'], 'L0_cond_scaling_factors': _L0_cond_in['scaling_factors'], 'L1_cond_base_weight': _L1_cond_in['base_weight'], 'L1_cond_base_bias': _L1_cond_in['base_bias'], 'L1_cond_lora_A_w': _L1_cond_in['lora_A_w'], 'L1_cond_lora_B_w': _L1_cond_in['lora_B_w'], 'L2_cond_weight': _L2_cond_in['weight'], 'L3_cond_weights': _L3_cond_in['weights']}

def reference(x, itok_B_1_7, itok_B_6_15, itok_B_3_7, itok_B_0_15, L0_cond_weight, L0_cond_bias, L0_cond_lora_a_weights, L0_cond_lora_b_weights, L0_cond_scaling_factors, L1_cond_base_weight, L1_cond_base_bias, L1_cond_lora_A_w, L1_cond_lora_B_w, L2_cond_weight, L3_cond_weights):
    import jax
    import jax.numpy as jnp

    def _L0_cond_ref(x, weight, bias, lora_a_weights, lora_b_weights, scaling_factors, adapter_id):
        import jax, jax.numpy as jnp
        import numpy as np
        B, S, D_IN, D_OUT = (4, 512, 1024, 1024)
        N_ADAPTERS, MAX_RANK = (8, 16)
        base = jnp.einsum('bsi,oi->bso', x, weight) + bias
        a_sel = lora_a_weights[adapter_id]
        b_sel = lora_b_weights[adapter_id]
        scale = scaling_factors[adapter_id]
        low = jnp.einsum('bsi,bri->bsr', x, a_sel)
        delta = jnp.einsum('bsr,bor->bso', low, b_sel)
        return base + scale[:, None, None] * delta

    def _L1_cond_ref(x, adapter_ids, base_weight, base_bias, lora_A_w, lora_B_w):
        import jax, jax.numpy as jnp
        import numpy as np
        B, S, D_IN, D_OUT = (4, 512, 1024, 1024)
        RANK, MAX_LORAS = (16, 32)
        result = jnp.einsum('bsd,od->bso', x, base_weight) + base_bias
        A = lora_A_w[adapter_ids]
        Bw = lora_B_w[adapter_ids]
        h = jnp.einsum('bsd,brd->bsr', x, A)
        lora_out = jnp.einsum('bsr,bor->bso', h, Bw)
        result = result + lora_out
        return result.astype(x.dtype)

    def _L2_cond_ref(x, weight, adapter_ids):
        import jax, jax.numpy as jnp
        import numpy as np
        MAX_LORAS, OUT, IN = (8, 1024, 1024)
        B, S = (4, 512)
        w = weight[adapter_ids]
        return jnp.einsum('bsi,boi->bso', x, w)

    def _L3_cond_ref(x, weights, condition):
        import jax, jax.numpy as jnp
        import numpy as np
        NUM_CONDITIONS = 16
        IN_CH = 64
        OUT_CH = 64
        B = 64
        T = 1024
        W = weights[condition]
        return jnp.einsum('bct,bcd->bdt', x, W)
    x = x + _L0_cond_ref(x, L0_cond_weight, L0_cond_bias, L0_cond_lora_a_weights, L0_cond_lora_b_weights, L0_cond_scaling_factors, itok_B_1_7)
    x = x + _L1_cond_ref(x, itok_B_6_15, L1_cond_base_weight, L1_cond_base_bias, L1_cond_lora_A_w, L1_cond_lora_B_w)
    x = x + _L2_cond_ref(x, L2_cond_weight, itok_B_3_7)
    x = x + _L3_cond_ref(x, L3_cond_weights, itok_B_0_15)
    return x

_drawn_inputs = setup_inputs


def setup_inputs(seed=0):
    import zlib

    import numpy as np

    out = dict(_drawn_inputs(seed))
    spreads = {}
    factors = {'L0_cond_bias': 8.0, 'L1_cond_base_bias': 8.0}
    for name, (base, spread) in spreads.items():
        noise = np.random.default_rng([zlib.crc32(name.encode()), seed]).standard_normal(out[name].shape)
        drawn = base * np.exp(spread * noise) if base else spread * noise
        out[name] = jnp.asarray(drawn.astype(out[name].dtype))
    for name, factor in factors.items():
        out[name] = (out[name] * factor).astype(out[name].dtype)
    return out
```

```python
from contextlib import ExitStack

import concourse.bass as bass
from concourse import mybir

F32 = mybir.dt.float32
F32R = mybir.dt.float32r
I32 = mybir.dt.int32
ALU = mybir.AluOpType
AX = mybir.AxisListType

P = 128
BATCHES, ROWS, FEATS = 32, 64, 1024
PAIRS = BATCHES // 2
KT = FEATS // P
HK = KT // 2
RANK = 16
MATS2 = 8
N_LORA0 = 8
BANK = 512
NB = FEATS // BANK
REPS = 3
KL = REPS * 2 * RANK
STAGES = 4
STEPS = 3 * PAIRS

SLOTS = BATCHES + 2
T_BATCH, T_COND, T_MAT, T_RANK = (n * SLOTS for n in range(4))
T_LORA = 4 * SLOTS
T_FACTS = T_LORA + 2 * BATCHES
T_MIXED = T_FACTS
T_ALL = T_MIXED + PAIRS
SLOT_OF = (1, 0)
LANDED = 16 * KT // STAGES
ORDER_STEPS = 18


def build(nc, xt, ids_cols, ids2_row, wt, bias, a_tab, b_tab, w3, out):
    ctx = ExitStack()
    with ctx:
        def sb(name, shape, dt):
            return ctx.enter_context(nc.sbuf_tensor(name, shape, dt))

        def psum(name, shape):
            return ctx.enter_context(nc.psum_tensor(name, shape, F32))

        def sem(name):
            return ctx.enter_context(nc.semaphore(name))

        x_all = sb("x_all", [P, PAIRS, 2, KT, ROWS], F32)
        w_ring = sb("w_ring", [P, 3, HK, 2, FEATS], F32R)
        w_stage = sb("w_stage", [P, STAGES, FEATS], F32)
        xs = sb("xs", [P, KT, 2, P], F32R)
        a_stage = sb("a_stage", [P, 2, KT, RANK], F32)
        a_split = sb("a_split", [P, KT, 2, KL], F32R)
        b_stage = sb("b_stage", [KL, FEATS + 1], F32)
        b_split = sb("b_split", [KL, FEATS], F32R)
        low_mask = sb("low_mask", [KL, P], F32)
        low_scale = sb("low_scale", [KL, P], F32)
        low_a = sb("low_a", [KL, P], F32)
        low_sum = sb("low_sum", [KL, P], F32)
        low_split = sb("low_split", [KL, P], F32R)
        rows = sb("rows", [P, 2, FEATS], F32)
        x3_hi = sb("x3_hi", [P, FEATS], F32R)
        x3_lo = sb("x3_lo", [P, FEATS], F32R)
        w3_stage = sb("w3_stage", [P, P], F32)
        w3_hi = sb("w3_hi", [P, P], F32R)
        w3_lo = sb("w3_lo", [P, P], F32R)
        bias_sb = sb("bias_sb", [P, 2, KT], F32)
        ident = sb("ident", [P, P], F32)
        B = BATCHES
        ids_i = sb("ids_i", [B, 4], I32)
        ids2_i = sb("ids2_i", [B, B], I32)
        ids2 = sb("ids2", [B, B], F32)
        num_col = sb("num_col", [B, 1], F32)
        num_row = sb("num_row", [B, SLOTS], F32)
        same = sb("same", [B, B], F32)
        less = sb("less", [B, B], F32)
        more = sb("more", [B, B], F32)
        counts = sb("counts", [B, 4], F32)
        one_hot = sb("one_hot", [B, SLOTS], F32)
        facts = sb("facts", [B, 6], F32)
        table = sb("table", [1, T_ALL], I32)

        y_ps = psum("y_ps", [P, 2, FEATS])
        t_ps = psum("t_ps", [P, FEATS])
        low_ps = psum("low_ps", [P, BANK])
        tab_ps = psum("tab_ps", [P, BANK])

        ids_in, bias_in = sem("ids_in"), sem("bias_in")
        x_in = [sem(f"x_in{n}") for n in range(2)]
        w_in = [sem(f"w_in{n}") for n in range(STAGES)]
        a_in, b_in, w3_in = sem("a_in"), sem("b_in"), sem("w3_in")
        stored = [sem(f"stored{n}") for n in range(2)]
        iota_ready, zeros_ready, ident_zero, ident_ready = (
            sem("iota_ready"), sem("zeros_ready"), sem("ident_zero"), sem("ident_ready"))
        order_step, order_mm, table_ready = sem("order_step"), sem("order_mm"), sem("table_ready")
        w_folded, w_hi, w_lo = sem("w_folded"), sem("w_hi"), sem("w_lo")
        hi_ready, lo_ready = sem("hi_ready"), sem("lo_ready")
        quarters = sem("quarters")
        low_step, low_ready = sem("low_step"), sem("low_ready")
        b_hi, b_lo = sem("b_hi"), sem("b_lo")
        y_done, y_taken = sem("y_done"), sem("y_taken")
        t_done, x_updated = sem("t_done"), sem("x_updated")
        x3_split, w3_hi_ready, w3_lo_ready = sem("x3_split"), sem("w3_hi_ready"), sem("w3_lo_ready")
        l3_done, out_ready = sem("l3_done"), sem("out_ready")

        def entry(eng, at, most):
            return eng.value_load(table[0:1, bass.ds(at, 1)], min_val=0, max_val=most)

        def rank_of(eng, j, slot):
            return entry(eng, 2 * j + (T_RANK + slot), MATS2 - 1)

        def ring_half(turn, h):
            return (2 * turn + h) % 3

        block = ctx.enter_context(nc.Block())

        @block.sync
        def _(sp):
            def load_chunk(matrix, k, turn):
                if not (isinstance(turn, int) and turn == 0 and k < STAGES):
                    sp.wait_ge(w_hi, turn * KT + (k - STAGES + 1))
                    sp.wait_ge(w_lo, turn * KT + (k - STAGES + 1))
                sp.dma_start(w_stage[:, k % STAGES, :], wt[matrix, k]).then_inc(w_in[k % STAGES], 16)

            def of_pair(start, at, most):
                return [entry(sp, at + (start + slot), most) for slot in SLOT_OF]

            def loras(t):
                return of_pair(T_LORA, 2 * t, a_tab.shape[0] - 1)

            def load_x(batches, p, parity):
                for b in range(2):
                    sp.dma_start(x_all[:, p, b].rearrange("p k r -> p (k r)"), xt[batches[b]]).then_inc(x_in[parity], 16)

            def load_a(which):
                for b in range(2):
                    sp.dma_start(a_stage[:, b].rearrange("p k r -> p (k r)"), a_tab[which[b]]).then_inc(a_in, 16)

            def load_b(which):
                for b in range(2):
                    for rep in range(REPS):
                        at = (2 * rep + b) * RANK
                        sp.dma_start(b_stage[at:at + RANK, :], b_tab[which[b]]).then_inc(b_in, 16)

            def load_w3(conds):
                for b in range(2):
                    r = slice(b * ROWS, (b + 1) * ROWS)
                    sp.dma_start(w3_stage[r, r], w3[conds[b]]).then_inc(w3_in, 16)

            def lora_step(t, parity, p=None, chunks=()):
                which = loras(t + 1)
                batches = None if p is None else of_pair(T_BATCH, 2 * p, BATCHES - 1)
                sp.wait_ge(hi_ready, 2 * t + 2)
                sp.wait_ge(lo_ready, 2 * t + 2)
                load_a(which)
                if p is not None:
                    if parity == 1:
                        sp.wait_ge(x_in[0], 16 * p)
                    elif not isinstance(p, int):
                        sp.wait_ge(x_in[1], 16 * p - 16)
                    load_x(batches, p, 1 - parity)
                for chunk in chunks:
                    load_chunk(*chunk)
                sp.wait_ge(b_hi, t + 1)
                sp.wait_ge(b_lo, t + 1)
                load_b(which)

            for n in range(2):
                sp.sem_inc(stored[n], 16)
            sp.dma_start(ids_i[:, :], ids_cols).then_inc(ids_in, 16)
            sp.dma_start(ids2_i[:, :], ids2_row.to_broadcast([BATCHES, BATCHES])).then_inc(ids_in, 16)
            for k in range(STAGES):
                load_chunk(0, k, 0)
            sp.dma_start(bias_sb[:, :, :], bias).then_inc(bias_in, 16)
            sp.wait_ge(table_ready, 1)
            load_x(of_pair(T_BATCH, 0, BATCHES - 1), 0, 0)
            load_a(loras(0))
            load_b(loras(0))
            for k in range(STAGES, KT):
                load_chunk(0, k, 0)

            lora_step(0, 0, p=1, chunks=[(1, k, 1) for k in range(STAGES)])
            with sp.Fori(0, PAIRS // 2 - 1) as i:
                lora_step(2 * i + 1, 1, p=2 * i + 2)
                lora_step(2 * i + 2, 0, p=2 * i + 3)
            lora_step(PAIRS - 1, 1, chunks=[(1, k, 1) for k in range(STAGES, KT)])

            matrix = entry(sp, T_MAT, MATS2 - 1) + 2
            lora_step(PAIRS, 0, chunks=[(matrix, k, 2) for k in range(STAGES)])
            with sp.Fori(0, PAIRS // 2 - 1) as i:
                lora_step(2 * i + (PAIRS + 1), 1)
                lora_step(2 * i + (PAIRS + 2), 0)
            sp.wait_ge(zeros_ready, 1)
            load_w3(of_pair(T_COND, 0, w3.shape[0] - 1))
            matrix = entry(sp, T_MAT, MATS2 - 1) + 2
            for k in range(STAGES, KT):
                load_chunk(matrix, k, 2)

            def store(batches, j, parity):
                sp.wait_ge(out_ready, j + 2)
                for b in range(2):
                    sp.dma_start(out[batches[b]], rows[b * ROWS:(b + 1) * ROWS, parity, :]).then_inc(stored[parity], 16)

            def switch_step(j, parity, first=False, last=False):
                ra, rb = rank_of(sp, j, 0), rank_of(sp, j, 1)
                matrix = entry(sp, 2 * j + (T_MAT + 1), MATS2 - 1)
                with sp.If(ra != rb):
                    for k in range(KT):
                        load_chunk(matrix + 2, k, rb + 2)
                if not last:
                    rn = rank_of(sp, j, 2)
                    matrix = entry(sp, 2 * j + (T_MAT + 2), MATS2 - 1)
                    with sp.If(rn != rb):
                        for k in range(KT):
                            load_chunk(matrix + 2, k, rn + 2)
                    conds = of_pair(T_COND, 2 * j + 2, w3.shape[0] - 1)
                if not first:
                    batches = of_pair(T_BATCH, 2 * j - 2, BATCHES - 1)
                if not last:
                    sp.wait_ge(w3_hi_ready, j + 1)
                    sp.wait_ge(w3_lo_ready, j + 1)
                    load_w3(conds)
                if not first:
                    store(batches, j - 1, 1 - parity)

            switch_step(0, 0, first=True)
            with sp.Fori(0, PAIRS // 2 - 1) as i:
                switch_step(2 * i + 1, 1)
                switch_step(2 * i + 2, 0)
            switch_step(PAIRS - 1, 1, last=True)
            store(of_pair(T_BATCH, BATCHES - 2, BATCHES - 1), PAIRS - 1, 1)
            for n in range(2):
                sp.wait_ge(stored[n], 16 + 16 * PAIRS)

        @block.gpsimd
        def _(pool):
            nc.gpsimd.iota(num_col[:, :], pattern=[[0, 1]], base=0, channel_multiplier=1,
                           allow_small_or_imprecise_dtypes=True).then_inc(iota_ready, 1)
            nc.gpsimd.iota(num_row[:, :], pattern=[[1, SLOTS]], base=0, channel_multiplier=0,
                           allow_small_or_imprecise_dtypes=True).then_inc(iota_ready, 1)
            nc.gpsimd.iota(low_a[:, :].bitcast(I32), pattern=[[0, P]], base=0, channel_multiplier=1).then_inc(iota_ready, 1)
            nc.gpsimd.iota(low_sum[:, :].bitcast(I32), pattern=[[1, 2], [0, ROWS]], base=0, channel_multiplier=0).then_inc(iota_ready, 1)
            nc.gpsimd.memset(w3_stage[:, :], 0.0).then_inc(zeros_ready, 1)
            nc.gpsimd.memset(ident[:, :], 0.0).then_inc(ident_zero, 1)
            pool.wait_ge(ident_zero, 1)
            nc.gpsimd.affine_select(out=ident[:, :], in_=ident[:, :], compare_op=ALU.not_equal, fill=1.0,
                                    base=0, pattern=[[-1, P]], channel_multiplier=1).then_inc(ident_ready, 1)
            pool.wait_ge(ident_ready, 1)

            def fold(r):
                for k in range(KT):
                    pool.wait_ge(w_in[k % STAGES], r * LANDED + (2 * LANDED + 16 * (k // STAGES + 1)))
                    diag = w_stage[:, k % STAGES, k * P:(k + 1) * P]
                    nc.gpsimd.tensor_tensor(diag, diag, ident[:, :], ALU.add).then_inc(w_folded, 1)

            fold(0)
            pool.wait_ge(table_ready, 1)
            with pool.Fori(0, PAIRS) as j:
                ra, rb, rn = (rank_of(pool, j, n) for n in range(3))
                with pool.If(ra != rb):
                    fold(rb)
                with pool.If(rn != rb):
                    fold(rn)

        def x_of(p, h):
            return x_all[:, p, :, h * HK:(h + 1) * HK, :].rearrange("p b k r -> p k b r")

        def xs_of(h, part):
            return xs[:, h * HK:(h + 1) * HK, part, :].rearrange("p k (b r) -> p k b r", b=2)

        def a_of(h, b):
            a = a_stage[:, b, h * HK:(h + 1) * HK, :]
            return a.unsqueeze(2).to_broadcast([P, HK, REPS, RANK])

        def a_split_of(h, part, b):
            a = a_split[:, h * HK:(h + 1) * HK, part, :].rearrange("p k (e b r) -> p k e b r", e=REPS, b=2)
            return a[:, :, :, b, :]

        @block.scalar
        def _(act):
            def convert(turn, h, half_at, rank=None):
                for k in range(h * HK, (h + 1) * HK):
                    if rank is None:
                        act.wait_ge(w_in[k % STAGES], turn * LANDED + 16 * (k // STAGES + 1))
                    else:
                        act.wait_ge(w_folded, rank * KT + (k + 1))
                    nc.scalar.copy(w_ring[:, half_at, k % HK, 0, :], w_stage[:, k % STAGES, :]).then_inc(w_hi, 1)

            def x_hi(s, p, h, lora):
                op = nc.scalar.copy(xs_of(h, 0), x_of(p, h))
                if lora:
                    act.wait_ge(a_in, 32 * s + 32)
                    for b in range(2):
                        op = nc.scalar.copy(a_split_of(h, 0, b), a_of(h, b))
                op.then_inc(hi_ready, 1)

            def wait_x(s, parity, layer0):
                if layer0:
                    act.wait_ge(x_in[parity], 16 * s + (32 if parity == 0 else 16))
                else:
                    act.wait_ge(x_updated, s - (PAIRS - 2))

            def take_y(t, parity):
                act.wait_ge(y_done, t + 2)
                act.wait_ge(t_done, t + 1)
                nc.scalar.copy(rows[:, parity, :], y_ps[:, parity, :]).then_inc(y_taken, 1)

            def lora_step(t, parity, p_next, first=False, following=None, layer0=False, lora=True):
                if following:
                    turn, rank = following
                    convert(turn, 0, ring_half(turn, 0), rank)
                if not first:
                    take_y(t - 1, 1 - parity)
                act.wait_ge(y_done, t + 1)
                act.wait_ge(b_in, 16 * 2 * REPS * t + 16 * 2 * REPS)
                nc.scalar.copy(b_split[:, :], b_stage[:, 0:FEATS]).then_inc(b_hi, 1)
                wait_x(t + 1, 1 - parity, layer0)
                act.wait_ge(quarters, 4 * t + 3)
                x_hi(t + 1, p_next, 0, lora)
                if following:
                    convert(turn, 1, ring_half(turn, 1), rank)
                act.wait_ge(quarters, 4 * t + 4)
                x_hi(t + 1, p_next, 1, lora)

            act.sem_inc(y_taken, 2)
            convert(0, 0, 0)
            wait_x(0, 0, True)
            x_hi(0, 0, 0, True)
            convert(0, 1, 1)
            x_hi(0, 0, 1, True)

            lora_step(0, 0, 1, first=True, layer0=True)
            with act.Fori(0, PAIRS // 2 - 1) as i:
                lora_step(2 * i + 1, 1, 2 * i + 2, layer0=True)
                lora_step(2 * i + 2, 0, 2 * i + 3, layer0=True)
            lora_step(PAIRS - 1, 1, 0, following=(1, None))

            lora_step(PAIRS, 0, 1)
            with act.Fori(0, PAIRS // 2 - 1) as i:
                lora_step(2 * i + (PAIRS + 1), 1, 2 * i + 2)
                lora_step(2 * i + (PAIRS + 2), 0, 2 * i + 3)
            lora_step(2 * PAIRS - 1, 1, 0, following=(2, 0), lora=False)

            def take_x3(j, parity):
                act.wait_ge(quarters, 4 * j + (4 * 2 * PAIRS + 4))
                act.wait_ge(l3_done, j + 1)
                act.wait_ge(stored[parity], 16 * j + (16 if parity == 0 else 0))
                nc.scalar.copy(x3_hi[:, :], y_ps[:, parity, :])
                nc.scalar.copy(rows[:, parity, :], y_ps[:, parity, :]).then_inc(y_taken, 1)

            def switch_step(j, parity, first=False, last=False):
                s4 = 4 * j + 4 * 2 * PAIRS
                if first:
                    take_y(2 * PAIRS - 1, 1)
                else:
                    take_x3(j - 1, 1 - parity)
                mixed, rb = entry(act, j + T_MIXED, 1), rank_of(act, j, 1)
                with act.If(mixed != 0):
                    convert(rb + 2, 0, ring_half(rb + 2, 0), rb)
                    act.wait_ge(quarters, s4 + 1)
                    convert(rb + 2, 1, ring_half(rb + 2, 1), rb)
                if not last:
                    rn = rank_of(act, j, 2)
                    with act.If(rn != rb):
                        act.wait_ge(quarters, s4 + 2 * mixed)
                        convert(rn + 2, 0, ring_half(rn + 2, 0), rn)
                act.wait_ge(w3_in, 32 * j + 32)
                act.wait_ge(l3_done, j + 1)
                nc.scalar.copy(w3_hi[:, :], w3_stage[:, :]).then_inc(w3_hi_ready, 1)
                if not last:
                    wait_x(j + (2 * PAIRS + 1), None, False)
                    act.wait_ge(quarters, s4 + 3)
                    x_hi(None, j + 1, 0, False)
                    with act.If(rn != rb):
                        convert(rn + 2, 1, ring_half(rn + 2, 1), rn)
                    act.wait_ge(quarters, s4 + 4)
                    x_hi(None, j + 1, 1, False)

            act.wait_ge(table_ready, 1)
            switch_step(0, 0, first=True)
            with act.Fori(0, PAIRS // 2 - 1) as i:
                switch_step(2 * i + 1, 1)
                switch_step(2 * i + 2, 0)
            switch_step(PAIRS - 1, 1, last=True)
            take_x3(PAIRS - 1, 1)

        @block.vector
        def _(dve):
            def order_the_batches():
                steps = [0]

                def then(op):
                    op.then_inc(order_step, 1)
                    steps[0] += 1

                def settled():
                    dve.wait_ge(order_step, steps[0])

                dve.wait_ge(ids_in, 32)
                dve.wait_ge(iota_ready, 4)
                then(nc.vector.tensor_copy(facts[:, 1:5], ids_i[:, :]))
                then(nc.vector.tensor_copy(ids2[:, :], ids2_i[:, :]))
                then(nc.vector.tensor_copy(facts[:, 0:1], num_col[:, :]))
                then(nc.vector.tensor_scalar(num_row[:, :], num_row[:, :], float(BATCHES - 1), None, ALU.min))
                mask_p, mask_r = low_a[:, :].bitcast(I32), low_sum[:, :].bitcast(I32)
                then(nc.vector.tensor_scalar(mask_p, mask_p, RANK.bit_length() - 1, 1, ALU.logical_shift_right,
                                             ALU.bitwise_and))
                settled()
                id2, numbers = facts[:, 2:3], num_row[:, 0:BATCHES]
                then(nc.vector.tensor_scalar(same[:, :], ids2[:, :], id2, None, ALU.is_equal))
                then(nc.vector.tensor_scalar(less[:, :], numbers, num_col[:, 0:1], None, ALU.is_lt))
                then(nc.vector.tensor_scalar(more[:, :], ids2[:, :], id2, None, ALU.is_gt))
                then(nc.vector.tensor_scalar(facts[:, 4:5], facts[:, 4:5], float(N_LORA0), None, ALU.add))
                then(nc.vector.tensor_tensor(low_mask[:, :], mask_p, mask_r, ALU.is_equal))
                settled()
                then(nc.vector.tensor_tensor(same[:, :], same[:, :], less[:, :], ALU.mult))
                settled()
                then(nc.vector.tensor_scalar(less[:, :], ids2[:, :], id2, None, ALU.is_lt))
                then(nc.vector.tensor_reduce(counts[:, 0:1], same[:, :], AX.X, ALU.add))
                settled()
                then(nc.vector.tensor_reduce(counts[:, 1:2], less[:, :], AX.X, ALU.add))
                then(nc.vector.tensor_scalar(counts[:, 3:4], counts[:, 0:1], 0.0, None, ALU.is_equal))
                settled()
                then(nc.vector.tensor_tensor(counts[:, 2:3], counts[:, 0:1], counts[:, 1:2], ALU.add))
                settled()
                then(nc.vector.tensor_scalar(one_hot[:, :], num_row[:, :], counts[:, 2:3], None, ALU.is_equal))
                dve.wait_ge(order_mm, 1)
                then(nc.vector.tensor_copy(facts[:, 5:6], tab_ps[0:BATCHES, BANK - 1:BANK]))
                dve.wait_ge(order_mm, 2)
                then(nc.vector.tensor_copy(table[:, 0:T_FACTS], tab_ps[0:1, 0:T_FACTS]))
                settled()
                ranks = table[:, T_RANK:T_RANK + BATCHES].rearrange("o (j s) -> o s j", s=2)
                nc.vector.tensor_tensor(table[:, T_MIXED:T_ALL], ranks[:, 1, :], ranks[:, 0, :],
                                        ALU.subtract).then_inc(table_ready, 1)
                assert steps[0] == ORDER_STEPS + 1

            def convert(turn, h, half_at):
                for k in range(h * HK, (h + 1) * HK):
                    dve.wait_ge(w_hi, turn * KT + (k + 1))
                    split = w_ring[:, half_at, k % HK]
                    nc.vector.tensor_tensor(split[:, 1, :], w_stage[:, k % STAGES, :], split[:, 0, :],
                                            ALU.subtract).then_inc(w_lo, 1)

            def x_lo(s, p, h, lora):
                dve.wait_ge(hi_ready, 2 * s + (h + 1))
                op = nc.vector.tensor_tensor(xs_of(h, 1), x_of(p, h), xs_of(h, 0), ALU.subtract)
                if lora:
                    for b in range(2):
                        op = nc.vector.tensor_tensor(a_split_of(h, 1, b), a_of(h, b), a_split_of(h, 0, b),
                                                     ALU.subtract)
                op.then_inc(lo_ready, 1)

            def low(t):
                dve.wait_ge(quarters, 4 * t + 4)
                dve.wait_ge(y_done, t + 1)
                dve.wait_ge(b_lo, t + 1)
                nc.vector.tensor_tensor(low_a[:, :], low_ps[0:KL, P:2 * P], low_scale[:, :], ALU.mult).then_inc(low_step, 1)
                nc.vector.tensor_tensor(low_sum[:, :], low_ps[0:KL, 0:P], low_scale[:, :], ALU.mult).then_inc(low_step, 1)
                dve.wait_ge(low_step, 4 * t + 2)
                nc.vector.tensor_tensor(low_sum[:, :], low_sum[:, :], low_a[:, :], ALU.add).then_inc(low_step, 1)
                dve.wait_ge(low_step, 4 * t + 3)
                nc.vector.tensor_copy(low_split[:, :], low_sum[:, :]).then_inc(low_step, 1)
                dve.wait_ge(low_step, 4 * t + 4)
                third = slice(2 * 2 * RANK, KL)
                nc.vector.tensor_tensor(low_split[third, :], low_sum[third, :], low_split[third, :],
                                        ALU.subtract).then_inc(low_ready, 1)

            def b_lo_part(t):
                dve.wait_ge(b_hi, t + 1)
                second = slice(2 * RANK, 2 * 2 * RANK)
                nc.vector.tensor_tensor(b_split[second, :], b_stage[second, 0:FEATS], b_split[second, :], ALU.subtract)
                nc.vector.tensor_scalar(low_scale[:, :], low_mask[:, :], b_stage[:, FEATS:FEATS + 1], None,
                                        ALU.mult).then_inc(b_lo, 1)

            def update_x(t, p, layer):
                dve.wait_ge(t_done, t + 3)
                for k in range(KT):
                    x = x_all[:, p, :, k, :]
                    op = nc.vector.scalar_tensor_tensor(
                        out=x, in0=t_ps[:, k * P:(k + 1) * P].rearrange("p (b r) -> p b r", b=2),
                        scalar=bias_sb[:, layer, k:k + 1], in1=x, op0=ALU.add, op1=ALU.add)
                op.then_inc(x_updated, 1)

            def lora_step(t, p, layer, first=False, second=False, updated=None, turn=None, lora=True):
                if not first:
                    low(t - 1)
                if updated:
                    update_x(t - 2, *updated)
                if turn is not None:
                    convert(turn, 0, ring_half(turn, 0))
                b_lo_part(t)
                p_next = p + 1 if turn is None else 0
                x_lo(t + 1, p_next, 0, lora)
                if turn is not None:
                    convert(turn, 1, ring_half(turn, 1))
                x_lo(t + 1, p_next, 1, lora)

            dve.sem_inc(low_ready, 1)
            dve.sem_inc(x_updated, 1)
            dve.sem_inc(out_ready, 1)
            order_the_batches()
            convert(0, 0, 0)
            x_lo(0, 0, 0, True)
            convert(0, 1, 1)
            x_lo(0, 0, 1, True)
            dve.wait_ge(bias_in, 16)

            lora_step(0, 0, 0, first=True)
            lora_step(1, 1, 0)
            with dve.Fori(2, PAIRS - 1) as t:
                lora_step(t, t, 0, updated=(t - 2, 0))
            lora_step(PAIRS - 1, PAIRS - 1, 0, updated=(PAIRS - 3, 0), turn=1)
            lora_step(PAIRS, 0, 1, updated=(PAIRS - 2, 0))
            lora_step(PAIRS + 1, 1, 1, updated=(PAIRS - 1, 0))
            with dve.Fori(2, PAIRS - 1) as p:
                lora_step(p + PAIRS, p, 1, updated=(p - 2, 1))
            lora_step(2 * PAIRS - 1, PAIRS - 1, 1, updated=(PAIRS - 3, 1), turn=2, lora=False)

            def x3_lo_part(j, parity):
                dve.wait_ge(y_taken, j + (2 * PAIRS + 3))
                dve.wait_ge(l3_done, j + 1)
                nc.vector.tensor_tensor(x3_lo[:, :], rows[:, parity, :], x3_hi[:, :], ALU.subtract).then_inc(x3_split, 1)

            def finish_out(j, parity):
                dve.wait_ge(l3_done, j + 2)
                nc.vector.tensor_tensor(rows[:, parity, :], t_ps[:, :], rows[:, parity, :], ALU.add).then_inc(out_ready, 1)

            def switch_step(j, parity, first=False, last=False):
                if first:
                    low(2 * PAIRS - 1)
                    update_x(2 * PAIRS - 2, PAIRS - 2, 1)
                else:
                    x3_lo_part(j - 1, 1 - parity)
                ra, rb = rank_of(dve, j, 0), rank_of(dve, j, 1)
                with dve.If(ra != rb):
                    convert(rb + 2, 0, ring_half(rb + 2, 0))
                    convert(rb + 2, 1, ring_half(rb + 2, 1))
                if not last:
                    rn = rank_of(dve, j, 2)
                    with dve.If(rn != rb):
                        convert(rn + 2, 0, ring_half(rn + 2, 0))
                if not first:
                    finish_out(j - 1, 1 - parity)
                dve.wait_ge(w3_hi_ready, j + 1)
                nc.vector.tensor_tensor(w3_lo[:, :], w3_stage[:, :], w3_hi[:, :], ALU.subtract).then_inc(w3_lo_ready, 1)
                if not last:
                    s = j + (2 * PAIRS + 1)
                    x_lo(s, j + 1, 0, False)
                    with dve.If(rn != rb):
                        convert(rn + 2, 1, ring_half(rn + 2, 1))
                    x_lo(s, j + 1, 1, False)

            switch_step(0, 0, first=True)
            update_x(2 * PAIRS - 1, PAIRS - 1, 1)
            with dve.Fori(0, PAIRS // 2 - 1) as i:
                switch_step(2 * i + 1, 1)
                switch_step(2 * i + 2, 0)
            switch_step(PAIRS - 1, 1, last=True)
            x3_lo_part(PAIRS - 1, 1)
            finish_out(PAIRS - 1, 1)

        @block.tensor
        def _(pe):
            def order_products():
                pe.wait_ge(order_step, ORDER_STEPS - 1)
                nc.tensor.matmul(tab_ps[0:BATCHES, BANK - 1:BANK], more[:, :], counts[:, 3:4],
                                 start=True, stop=True).then_inc(order_mm, 1)
                pe.wait_ge(order_step, ORDER_STEPS)
                for fact, at, n in ((0, T_BATCH, SLOTS), (1, T_COND, SLOTS), (2, T_MAT, SLOTS), (5, T_RANK, SLOTS),
                                    (3, T_LORA, BATCHES), (4, T_LORA + BATCHES, BATCHES)):
                    op = nc.tensor.matmul(tab_ps[0:1, at:at + n], facts[:, fact:fact + 1], one_hot[:, 0:n],
                                          start=True, stop=True)
                op.then_inc(order_mm, 1)

            def half(h, parity, half_at, m=P, lora=False, stop=True, each_tile=None, marks=()):
                for k in range(h * HK, (h + 1) * HK):
                    if each_tile is not None:
                        pe.wait_ge(w_lo, each_tile + k + 1)
                    for part_x, part_w in ((0, 0), (0, 1), (1, 0)):
                        for n in range(NB):
                            cols = slice(n * BANK, (n + 1) * BANK)
                            op = nc.tensor.matmul(
                                y_ps[0:m, parity, cols], xs[:, k, part_x, 0:m], w_ring[:, half_at, k % HK, part_w, cols],
                                start=k == 0 and part_x == part_w, stop=stop and k == KT - 1 and part_x == 1)
                    if lora:
                        nc.tensor.matmul(low_ps[0:KL, 0:2 * P], a_split[:, k, 0, :],
                                         xs[:, k].rearrange("p s r -> p (s r)"), start=k == 0, stop=False)
                        op = nc.tensor.matmul(low_ps[0:KL, 0:P], a_split[:, k, 1, :], xs[:, k, 0, :],
                                              start=False, stop=k == KT - 1)
                    if k in marks:
                        op.then_inc(quarters, 1)

            def lora_b(t, parity):
                pe.wait_ge(low_ready, t + 2)
                pe.wait_ge(b_lo, t + 1)
                for n in range(NB):
                    cols = slice(n * BANK, (n + 1) * BANK)
                    op = nc.tensor.matmul(y_ps[:, parity, cols], low_split[:, :], b_split[:, cols], start=False, stop=True)
                op.then_inc(y_done, 1)

            def transposes(t, parity):
                pe.wait_ge(y_taken, t + 3)
                pe.wait_ge(x_updated, t + 1)
                for k in range(KT):
                    cols = slice(k * P, (k + 1) * P)
                    op = nc.tensor.transpose(t_ps[:, cols], rows[:, parity, cols], ident[:, :])
                op.then_inc(t_done, 1)

            def operands(s, h):
                pe.wait_ge(hi_ready, 2 * s + (h + 1))
                pe.wait_ge(lo_ready, 2 * s + (h + 1))

            MARKS = (HK - 3, HK - 2, HK - 1, KT - 1)

            def lora_step(t, parity, turn, first=False):
                pe.wait_ge(y_taken, t + 1)
                pe.wait_ge(low_ready, t + 1)
                operands(t, 0)
                pe.wait_ge(w_lo, turn * KT + (1 if first else HK))
                half(0, parity, ring_half(turn, 0), lora=True, stop=False, each_tile=turn * KT if first else None, marks=MARKS)
                if not first:
                    lora_b(t - 1, 1 - parity)
                operands(t, 1)
                if not first:
                    pe.wait_ge(w_lo, turn * KT + KT)
                half(1, parity, ring_half(turn, 1), lora=True, stop=False, each_tile=turn * KT if first else None, marks=MARKS)
                if not first:
                    transposes(t - 1, 1 - parity)

            pe.sem_inc(y_done, 1)
            pe.sem_inc(t_done, 2)
            pe.sem_inc(l3_done, 1)
            order_products()
            pe.wait_ge(ident_ready, 1)
            for layer in range(2):
                s = layer * PAIRS
                lora_step(s, 0, layer, first=layer == 0)
                with pe.Fori(0, PAIRS // 2 - 1) as i:
                    lora_step(2 * i + (s + 1), 1, layer)
                    lora_step(2 * i + (s + 2), 0, layer)
                lora_step(s + PAIRS - 1, 1, layer)

            def layer3(j, parity):
                pe.wait_ge(x3_split, j + 1)
                pe.wait_ge(w3_lo_ready, j + 1)
                pe.wait_ge(out_ready, j + 1)
                for w, x in ((w3_hi, x3_hi), (w3_hi, x3_lo), (w3_lo, x3_hi)):
                    for n in range(NB):
                        cols = slice(n * BANK, (n + 1) * BANK)
                        op = nc.tensor.matmul(t_ps[:, cols], w[:, :], x[:, cols],
                                              start=w is w3_hi and x is x3_hi, stop=w is w3_lo)
                op.then_inc(l3_done, 1)

            def switch_step(j, parity, first=False):
                s = j + 2 * PAIRS
                ra, rb = rank_of(pe, j, 0), rank_of(pe, j, 1)
                pe.wait_ge(y_taken, s + 1)
                operands(s, 0)
                pe.wait_ge(w_lo, ra * KT + (2 * KT + HK))
                a_half, b_half = (tuple(ring_half(r + 2, h) for h in range(2)) for r in (ra, rb))
                with pe.If(ra != rb):
                    half(0, parity, a_half[0], marks=(HK - 1,))
                with pe.Else():
                    half(0, parity, a_half[0], marks=MARKS)
                if first:
                    lora_b(2 * PAIRS - 1, 1)
                else:
                    layer3(j - 1, 1 - parity)
                operands(s, 1)
                pe.wait_ge(w_lo, ra * KT + (2 * KT + KT))
                with pe.If(ra != rb):
                    half(1, parity, a_half[1], marks=(KT - 1,))
                    pe.wait_ge(w_lo, rb * KT + (2 * KT + HK))
                    half(0, parity, b_half[0], m=ROWS, marks=(HK - 1,))
                    pe.wait_ge(w_lo, rb * KT + (2 * KT + KT))
                    half(1, parity, b_half[1], m=ROWS, marks=(KT - 1,))
                with pe.Else():
                    half(1, parity, a_half[1], marks=MARKS)
                if first:
                    transposes(2 * PAIRS - 1, 1)

            pe.wait_ge(table_ready, 1)
            switch_step(0, 0, first=True)
            pe.wait_ge(x_updated, 2 * PAIRS + 1)
            with pe.Fori(0, PAIRS // 2 - 1) as i:
                switch_step(2 * i + 1, 1)
                switch_step(2 * i + 2, 0)
            switch_step(PAIRS - 1, 1)
            layer3(PAIRS - 1, 1)


def kernel(x, itok_B_1_7, itok_B_6_15, itok_B_3_7, itok_B_0_15, L0_cond_weight, L0_cond_bias,
           L0_cond_lora_a_weights, L0_cond_lora_b_weights, L0_cond_scaling_factors, L1_cond_base_weight,
           L1_cond_base_bias, L1_cond_lora_A_w, L1_cond_lora_B_w, L2_cond_weight, L3_cond_weights):
    import numpy as np
    import concourse.bacc as bacc
    from concourse.bass_utils import run_bass_kernel_spmd

    def arr(a):
        return np.asarray(a)

    def a_layout(a):
        n = a.shape[0]
        return arr(a).reshape(n, RANK, KT, P).transpose(0, 3, 2, 1).reshape(n, P, KT * RANK)

    def b_layout(b, scale):
        n = b.shape[0]
        scale = np.broadcast_to(arr(scale)[:, None, None], (n, RANK, 1))
        return np.concatenate([arr(b).transpose(0, 2, 1), scale], axis=2)

    ids = np.stack([arr(i) for i in (itok_B_0_15, itok_B_3_7, itok_B_1_7, itok_B_6_15)], axis=1)
    weights = np.concatenate([arr(L0_cond_weight)[None], arr(L1_cond_base_weight)[None], arr(L2_cond_weight)])
    ones = np.ones(L1_cond_lora_A_w.shape[0], np.float32)
    arrays = {
        "xt": arr(x).reshape(BATCHES, ROWS, KT, P).transpose(0, 3, 2, 1).reshape(BATCHES, P, KT * ROWS),
        "ids_cols": ids.astype(np.int32),
        "ids2_row": arr(itok_B_3_7).reshape(1, BATCHES).astype(np.int32),
        "wt": weights.transpose(0, 2, 1).reshape(2 + MATS2, KT, P, FEATS),
        "bias": np.stack([arr(L0_cond_bias), arr(L1_cond_base_bias)]).reshape(2, KT, P).transpose(2, 0, 1),
        "a_tab": np.concatenate([a_layout(L0_cond_lora_a_weights), a_layout(L1_cond_lora_A_w)]),
        "b_tab": np.concatenate([b_layout(L0_cond_lora_b_weights, L0_cond_scaling_factors),
                                 b_layout(L1_cond_lora_B_w, ones)]),
        "w3": arr(L3_cond_weights),
    }
    arrays = {name: np.ascontiguousarray(a) for name, a in arrays.items()}
    nc = bacc.Bacc("TRN2", target_bir_lowering=False, num_devices=1, dynamic_dma_scratch_size=1024)
    args = {name: nc.dram_tensor(name, a.shape, mybir.dt.from_np(a.dtype), kind="ExternalInput").ap()
            for name, a in arrays.items()}
    out = nc.dram_tensor("out", (BATCHES, ROWS, FEATS), F32, kind="ExternalOutput").ap()
    build(nc, out=out, **args)
    return run_bass_kernel_spmd(nc, [arrays], core_ids=[0]).results[0]["out"]
```

```python
from contextlib import ExitStack

import concourse.bass as bass
from concourse import mybir

F32 = mybir.dt.float32
F32R = mybir.dt.float32r
I32 = mybir.dt.int32
ALU = mybir.AluOpType
AX = mybir.AxisListType

P = 128
BATCHES, ROWS, FEATS = 32, 64, 1024
PAIRS = BATCHES // 2
KT = FEATS // P
HK = KT // 2
RANK = 16
MATS2 = 8
N_LORA0 = 8
BANK = 512
NB = FEATS // BANK
GROUPS = 4
GROUP = 2 * RANK
KL = GROUPS * GROUP
STAGES = 4
STEPS = 3 * PAIRS

SLOTS = BATCHES + 2
T_BATCH, T_COND, T_MAT, T_RANK = (n * SLOTS for n in range(4))
T_LORA = 4 * SLOTS
T_USED = T_LORA + 2 * BATCHES
T_FACTS = T_USED + MATS2 + 1
T_MIXED = T_FACTS
T_ALL = T_MIXED + PAIRS
SLOT_OF = (1, 0)
LANDED = 16 * KT // STAGES
ORDER_SAME, ORDER_RANK, ORDER_STEPS = 6, 24, 26


def build(nc, xt, ids_cols, ids2_row, wt, bias, a_tab, b_tab, w3, out):
    ctx = ExitStack()
    with ctx:
        def sb(name, shape, dt):
            return ctx.enter_context(nc.sbuf_tensor(name, shape, dt))

        def psum(name, shape):
            return ctx.enter_context(nc.psum_tensor(name, shape, F32))

        def sem(name):
            return ctx.enter_context(nc.semaphore(name))

        x_all = sb("x_all", [P, PAIRS, 2, KT, ROWS], F32)
        w_ring = sb("w_ring", [P, 3, HK, 2, FEATS], F32R)
        w_stage = sb("w_stage", [P, STAGES, FEATS], F32)
        xs = sb("xs", [P, KT, 2, P], F32R)
        a_stage = sb("a_stage", [P, 2, KT, RANK], F32)
        a_split = sb("a_split", [P, KT, KL], F32R)
        b_stage = sb("b_stage", [KL, FEATS + 1], F32)
        b_split = sb("b_split", [KL, FEATS], F32R)
        low_mask = sb("low_mask", [KL, P], F32)
        low_scale = sb("low_scale", [KL, P], F32)
        low_a = sb("low_a", [KL, P], F32)
        low_sum = sb("low_sum", [KL, P], F32)
        low_split = sb("low_split", [KL, P], F32R)
        rows = sb("rows", [P, 2, FEATS], F32)
        x3_hi = sb("x3_hi", [P, FEATS], F32R)
        x3_lo = sb("x3_lo", [P, FEATS], F32R)
        w3_stage = sb("w3_stage", [P, P], F32)
        w3_hi = sb("w3_hi", [P, P], F32R)
        w3_lo = sb("w3_lo", [P, P], F32R)
        bias_sb = sb("bias_sb", [P, 2, KT], F32)
        ident = sb("ident", [P, P], F32)
        B = BATCHES
        ids_i = sb("ids_i", [B, 4], I32)
        ids2_i = sb("ids2_i", [B, B], I32)
        ids2 = sb("ids2", [B, B], F32)
        num_col = sb("num_col", [B, 1], F32)
        num_row = sb("num_row", [B, SLOTS], F32)
        group = sb("group", [B, B + 1], I32)
        keys = sb("keys", [B, B + 1], F32)
        ones = sb("ones", [B, B], F32)
        same = sb("same", [B, B], F32)
        less = sb("less", [B, B], F32)
        more = sb("more", [B, B], F32)
        counts = sb("counts", [B, 4], F32)
        one_hot = sb("one_hot", [B, SLOTS], F32)
        rank_hot = sb("rank_hot", [B, MATS2 + 1], F32)
        facts = sb("facts", [B, 6], F32)
        table = sb("table", [1, T_ALL], I32)

        y_ps = psum("y_ps", [P, 2, FEATS])
        t_ps = psum("t_ps", [P, FEATS])
        low_ps = psum("low_ps", [P, 2, BANK])
        tab_ps = low_ps[:, 1, :]

        ids_in, bias_in = sem("ids_in"), sem("bias_in")
        x_in = [sem(f"x_in{n}") for n in range(2)]
        w_in = [sem(f"w_in{n}") for n in range(STAGES)]
        a_in, b_in, w3_in = sem("a_in"), sem("b_in"), sem("w3_in")
        stored = [sem(f"stored{n}") for n in range(2)]
        iota_ready, zeros_ready, ident_zero, ident_ready = (
            sem("iota_ready"), sem("zeros_ready"), sem("ident_zero"), sem("ident_ready"))
        order_step, order_mm, table_ready = sem("order_step"), sem("order_mm"), sem("table_ready")
        w_folded, w_hi, w_lo = sem("w_folded"), sem("w_hi"), sem("w_lo")
        x_hi_ready, x_lo_ready = sem("x_hi_ready"), sem("x_lo_ready")
        a_hi_ready, a_lo_ready = sem("a_hi_ready"), sem("a_lo_ready")
        quarters = sem("quarters")
        low_step, low_ready = sem("low_step"), sem("low_ready")
        b_hi, b_lo = sem("b_hi"), sem("b_lo")
        y_done, y_taken = sem("y_done"), sem("y_taken")
        t_done, x_updated = sem("t_done"), sem("x_updated")
        x3_split, w3_hi_ready, w3_lo_ready = sem("x3_split"), sem("w3_hi_ready"), sem("w3_lo_ready")
        l3_done, out_ready = sem("l3_done"), sem("out_ready")

        def entry(eng, at, most):
            return eng.value_load(table[0:1, bass.ds(at, 1)], min_val=0, max_val=most)

        def rank_of(eng, j, slot):
            return entry(eng, 2 * j + (T_RANK + slot), MATS2 - 1)

        def ring_half(turn, h):
            return (2 * turn + h) % 3

        block = ctx.enter_context(nc.Block())

        @block.sync
        def _(sp):
            def load_chunk(matrix, k, turn):
                if not (isinstance(turn, int) and turn == 0 and k < STAGES):
                    sp.wait_ge(w_hi, turn * KT + (k - STAGES + 1))
                    sp.wait_ge(w_lo, turn * KT + (k - STAGES + 1))
                sp.dma_start(w_stage[:, k % STAGES, :], wt[matrix, k]).then_inc(w_in[k % STAGES], 16)

            def of_pair(start, at, most):
                return [entry(sp, at + (start + slot), most) for slot in SLOT_OF]

            def loras(t):
                return of_pair(T_LORA, 2 * t, a_tab.shape[0] - 1)

            def load_x(batches, p, parity):
                for b in range(2):
                    sp.dma_start(x_all[:, p, b].rearrange("p k r -> p (k r)"), xt[batches[b]]).then_inc(x_in[parity], 16)

            def load_a(which):
                for b in range(2):
                    sp.dma_start(a_stage[:, b].rearrange("p k r -> p (k r)"), a_tab[which[b]]).then_inc(a_in, 16)

            def load_b(which):
                for b in range(2):
                    for rep in range(GROUPS):
                        at = rep * GROUP + b * RANK
                        sp.dma_start(b_stage[at:at + RANK, :], b_tab[which[b]]).then_inc(b_in, 16)

            def load_w3(conds):
                for b in range(2):
                    r = slice(b * ROWS, (b + 1) * ROWS)
                    sp.dma_start(w3_stage[r, r], w3[conds[b]]).then_inc(w3_in, 16)

            def lora_step(t, parity, p=None, chunks=()):
                which = loras(t + 1)
                batches = None if p is None else of_pair(T_BATCH, 2 * p, BATCHES - 1)
                sp.wait_ge(a_hi_ready, 2 * t + 2)
                sp.wait_ge(a_lo_ready, 2 * t + 2)
                load_a(which)
                if p is not None:
                    if parity == 1:
                        sp.wait_ge(x_in[0], 16 * p)
                    elif not isinstance(p, int):
                        sp.wait_ge(x_in[1], 16 * p - 16)
                    load_x(batches, p, 1 - parity)
                for chunk in chunks:
                    load_chunk(*chunk)
                sp.wait_ge(b_hi, t + 1)
                sp.wait_ge(b_lo, t + 1)
                load_b(which)

            for n in range(2):
                sp.sem_inc(stored[n], 16)
            sp.dma_start(ids_i[:, :], ids_cols).then_inc(ids_in, 16)
            sp.dma_start(ids2_i[:, :], ids2_row.to_broadcast([BATCHES, BATCHES])).then_inc(ids_in, 16)
            for k in range(STAGES):
                load_chunk(0, k, 0)
            sp.dma_start(bias_sb[:, :, :], bias).then_inc(bias_in, 16)
            sp.wait_ge(table_ready, 1)
            load_x(of_pair(T_BATCH, 0, BATCHES - 1), 0, 0)
            load_a(loras(0))
            for k in range(STAGES, KT):
                load_chunk(0, k, 0)
            load_b(loras(0))

            lora_step(0, 0, p=1, chunks=[(1, k, 1) for k in range(STAGES)])
            with sp.Fori(0, PAIRS // 2 - 1) as i:
                lora_step(2 * i + 1, 1, p=2 * i + 2)
                lora_step(2 * i + 2, 0, p=2 * i + 3)
            lora_step(PAIRS - 1, 1, chunks=[(1, k, 1) for k in range(STAGES, KT)])

            def first_chunks(rank):
                used = entry(sp, rank + T_USED, MATS2)
                with sp.If(used != 0):
                    for k in range(STAGES):
                        load_chunk(used + 1, k, rank + 2)

            def other_chunks(rank):
                used = entry(sp, rank + T_USED, MATS2)
                for k in range(STAGES, KT):
                    load_chunk(used + 1, k, rank + 2)

            matrix = entry(sp, T_MAT, MATS2 - 1) + 2
            lora_step(PAIRS, 0, chunks=[(matrix, k, 2) for k in range(STAGES)])
            with sp.Fori(0, PAIRS // 2 - 1) as i:
                lora_step(2 * i + (PAIRS + 1), 1)
                lora_step(2 * i + (PAIRS + 2), 0)
            sp.wait_ge(zeros_ready, 1)
            load_w3(of_pair(T_COND, 0, w3.shape[0] - 1))
            other_chunks(0)
            first_chunks(1)

            def store(batches, j, parity):
                sp.wait_ge(out_ready, j + 2)
                for b in range(2):
                    sp.dma_start(out[batches[b]], rows[b * ROWS:(b + 1) * ROWS, parity, :]).then_inc(stored[parity], 16)

            def switch_step(j, parity, first=False, last=False):
                ra, rb = rank_of(sp, j, 0), rank_of(sp, j, 1)
                with sp.If(ra != rb):
                    other_chunks(rb)
                    first_chunks(rb + 1)
                if not last:
                    rn = rank_of(sp, j, 2)
                    with sp.If(rn != rb):
                        other_chunks(rn)
                        first_chunks(rn + 1)
                    conds = of_pair(T_COND, 2 * j + 2, w3.shape[0] - 1)
                if not first:
                    batches = of_pair(T_BATCH, 2 * j - 2, BATCHES - 1)
                if not last:
                    sp.wait_ge(w3_hi_ready, j + 1)
                    sp.wait_ge(w3_lo_ready, j + 1)
                    load_w3(conds)
                if not first:
                    store(batches, j - 1, 1 - parity)

            switch_step(0, 0, first=True)
            with sp.Fori(0, PAIRS // 2 - 1) as i:
                switch_step(2 * i + 1, 1)
                switch_step(2 * i + 2, 0)
            switch_step(PAIRS - 1, 1, last=True)
            store(of_pair(T_BATCH, BATCHES - 2, BATCHES - 1), PAIRS - 1, 1)
            for n in range(2):
                sp.wait_ge(stored[n], 16 + 16 * PAIRS)

        @block.gpsimd
        def _(pool):
            nc.gpsimd.iota(num_col[:, :], pattern=[[0, 1]], base=0, channel_multiplier=1,
                           allow_small_or_imprecise_dtypes=True).then_inc(iota_ready, 1)
            nc.gpsimd.iota(num_row[:, :], pattern=[[1, SLOTS]], base=0, channel_multiplier=0,
                           allow_small_or_imprecise_dtypes=True).then_inc(iota_ready, 1)
            nc.gpsimd.iota(low_a[:, :].bitcast(I32), pattern=[[0, P]], base=0, channel_multiplier=1).then_inc(iota_ready, 1)
            nc.gpsimd.iota(low_sum[:, :].bitcast(I32), pattern=[[1, 2], [0, ROWS]], base=0, channel_multiplier=0).then_inc(iota_ready, 1)
            nc.gpsimd.memset(ones[:, :], 1.0).then_inc(iota_ready, 1)
            nc.gpsimd.memset(w3_stage[:, :], 0.0).then_inc(zeros_ready, 1)
            nc.gpsimd.memset(ident[:, :], 0.0).then_inc(ident_zero, 1)
            pool.wait_ge(ident_zero, 1)
            nc.gpsimd.affine_select(out=ident[:, :], in_=ident[:, :], compare_op=ALU.not_equal, fill=1.0,
                                    base=0, pattern=[[-1, P]], channel_multiplier=1).then_inc(ident_ready, 1)
            pool.wait_ge(ident_ready, 1)

            def fold(r):
                for k in range(KT):
                    pool.wait_ge(w_in[k % STAGES], r * LANDED + (2 * LANDED + 16 * (k // STAGES + 1)))
                    diag = w_stage[:, k % STAGES, k * P:(k + 1) * P]
                    nc.gpsimd.tensor_tensor(diag, diag, ident[:, :], ALU.add).then_inc(w_folded, 1)

            fold(0)
            pool.wait_ge(table_ready, 1)
            with pool.Fori(0, PAIRS) as j:
                ra, rb, rn = (rank_of(pool, j, n) for n in range(3))
                with pool.If(ra != rb):
                    fold(rb)
                with pool.If(rn != rb):
                    fold(rn)

        def x_of(p, h):
            return x_all[:, p, :, h * HK:(h + 1) * HK, :].rearrange("p b k r -> p k b r")

        def xs_of(h, part):
            return xs[:, h * HK:(h + 1) * HK, part, :].rearrange("p k (b r) -> p k b r", b=2)

        def a_of(h, b):
            return a_stage[:, b, h * HK:(h + 1) * HK, :]

        def a_split_of(h, b):
            a = a_split[:, h * HK:(h + 1) * HK, :].rearrange("p k (e b r) -> p k e b r", e=GROUPS, b=2)
            return a[:, :, :, b, :]

        @block.scalar
        def _(act):
            def convert(turn, h, half_at, rank=None):
                for k in range(h * HK, (h + 1) * HK):
                    if rank is None:
                        act.wait_ge(w_in[k % STAGES], turn * LANDED + 16 * (k // STAGES + 1))
                    else:
                        act.wait_ge(w_folded, rank * KT + (k + 1))
                    nc.scalar.copy(w_ring[:, half_at, k % HK, 0, :], w_stage[:, k % STAGES, :]).then_inc(w_hi, 1)

            def x_hi(s, p, h, lora):
                nc.scalar.copy(xs_of(h, 0), x_of(p, h)).then_inc(x_hi_ready, 1)
                if lora:
                    act.wait_ge(a_in, 32 * s + 32)
                    for b in range(2):
                        op = nc.scalar.copy(a_split_of(h, b)[:, :, 0:GROUPS - 1, :],
                                            a_of(h, b).unsqueeze(2).to_broadcast([P, HK, GROUPS - 1, RANK]))
                    op.then_inc(a_hi_ready, 1)

            def wait_x(s, parity, layer0):
                if layer0:
                    act.wait_ge(x_in[parity], 16 * s + (32 if parity == 0 else 16))
                else:
                    act.wait_ge(x_updated, s - (PAIRS - 2))

            def take_y(t, parity):
                act.wait_ge(y_done, t + 2)
                act.wait_ge(t_done, t + 1)
                nc.scalar.copy(rows[:, parity, :], y_ps[:, parity, :]).then_inc(y_taken, 1)

            def lora_step(t, parity, p_next, first=False, following=None, layer0=False, lora=True):
                if following:
                    turn, rank = following
                    convert(turn, 0, ring_half(turn, 0), rank)
                if not first:
                    take_y(t - 1, 1 - parity)
                act.wait_ge(y_done, t + 1)
                act.wait_ge(b_in, 16 * 2 * GROUPS * t + 16 * 2 * GROUPS)
                nc.scalar.copy(b_split[:, :], b_stage[:, 0:FEATS]).then_inc(b_hi, 1)
                wait_x(t + 1, 1 - parity, layer0)
                act.wait_ge(quarters, 4 * t + 3)
                x_hi(t + 1, p_next, 0, lora)
                if following:
                    convert(turn, 1, ring_half(turn, 1), rank)
                act.wait_ge(quarters, 4 * t + 4)
                x_hi(t + 1, p_next, 1, lora)

            act.sem_inc(y_taken, 2)
            convert(0, 0, 0)
            wait_x(0, 0, True)
            x_hi(0, 0, 0, True)
            convert(0, 1, 1)
            x_hi(0, 0, 1, True)

            lora_step(0, 0, 1, first=True, layer0=True)
            with act.Fori(0, PAIRS // 2 - 1) as i:
                lora_step(2 * i + 1, 1, 2 * i + 2, layer0=True)
                lora_step(2 * i + 2, 0, 2 * i + 3, layer0=True)
            lora_step(PAIRS - 1, 1, 0, following=(1, None))

            lora_step(PAIRS, 0, 1)
            with act.Fori(0, PAIRS // 2 - 1) as i:
                lora_step(2 * i + (PAIRS + 1), 1, 2 * i + 2)
                lora_step(2 * i + (PAIRS + 2), 0, 2 * i + 3)
            lora_step(2 * PAIRS - 1, 1, 0, following=(2, 0), lora=False)

            def take_x3(j, parity):
                act.wait_ge(quarters, 4 * j + (4 * 2 * PAIRS + 4))
                act.wait_ge(l3_done, j + 1)
                act.wait_ge(stored[parity], 16 * j + (16 if parity == 0 else 0))
                nc.scalar.copy(x3_hi[:, :], y_ps[:, parity, :])
                nc.scalar.copy(rows[:, parity, :], y_ps[:, parity, :]).then_inc(y_taken, 1)

            def switch_step(j, parity, first=False, last=False):
                s4 = 4 * j + 4 * 2 * PAIRS
                if first:
                    take_y(2 * PAIRS - 1, 1)
                else:
                    take_x3(j - 1, 1 - parity)
                mixed, rb = entry(act, j + T_MIXED, 1), rank_of(act, j, 1)
                with act.If(mixed != 0):
                    convert(rb + 2, 0, ring_half(rb + 2, 0), rb)
                    act.wait_ge(quarters, s4 + 1)
                    convert(rb + 2, 1, ring_half(rb + 2, 1), rb)
                if not last:
                    rn = rank_of(act, j, 2)
                    with act.If(rn != rb):
                        act.wait_ge(quarters, s4 + 2 * mixed)
                        convert(rn + 2, 0, ring_half(rn + 2, 0), rn)
                act.wait_ge(w3_in, 32 * j + 32)
                act.wait_ge(l3_done, j + 1)
                nc.scalar.copy(w3_hi[:, :], w3_stage[:, :]).then_inc(w3_hi_ready, 1)
                if not last:
                    wait_x(j + (2 * PAIRS + 1), None, False)
                    act.wait_ge(quarters, s4 + 3)
                    x_hi(None, j + 1, 0, False)
                    with act.If(rn != rb):
                        convert(rn + 2, 1, ring_half(rn + 2, 1), rn)
                    act.wait_ge(quarters, s4 + 4)
                    x_hi(None, j + 1, 1, False)

            act.wait_ge(table_ready, 1)
            switch_step(0, 0, first=True)
            with act.Fori(0, PAIRS // 2 - 1) as i:
                switch_step(2 * i + 1, 1)
                switch_step(2 * i + 2, 0)
            switch_step(PAIRS - 1, 1, last=True)
            take_x3(PAIRS - 1, 1)

        @block.vector
        def _(dve):
            def order_the_batches():
                steps = [0]

                def then(op):
                    op.then_inc(order_step, 1)
                    steps[0] += 1

                def settled():
                    dve.wait_ge(order_step, steps[0])

                dve.wait_ge(ids_in, 32)
                dve.wait_ge(iota_ready, 4)
                then(nc.vector.tensor_copy(facts[:, 1:5], ids_i[:, :]))
                then(nc.vector.tensor_copy(ids2[:, :], ids2_i[:, :]))
                then(nc.vector.tensor_copy(facts[:, 0:1], num_col[:, :]))
                then(nc.vector.tensor_scalar(num_row[:, :], num_row[:, :], float(BATCHES - 1), None, ALU.min))
                mask_p, mask_r = low_a[:, :].bitcast(I32), low_sum[:, :].bitcast(I32)
                then(nc.vector.tensor_scalar(mask_p, mask_p, RANK.bit_length() - 1, 1, ALU.logical_shift_right,
                                             ALU.bitwise_and))
                settled()
                id2, numbers = facts[:, 2:3], num_row[:, 0:BATCHES]
                then(nc.vector.tensor_scalar(same[:, :], ids2[:, :], id2, None, ALU.is_equal))
                settled()
                then(nc.vector.tensor_reduce(counts[:, 0:1], same[:, :], AX.X, ALU.add))
                dve.wait_ge(order_mm, 1)
                then(nc.vector.tensor_copy(group[:, 0:BATCHES], tab_ps[0:BATCHES, 0:BATCHES]))
                settled()
                then(nc.vector.tensor_copy(group[:, BATCHES:], counts[:, 0:1]))
                settled()
                then(nc.vector.tensor_scalar(group[:, :], group[:, :], 1, MATS2.bit_length() - 1,
                                             ALU.bitwise_and, ALU.logical_shift_left))
                settled()
                then(nc.vector.tensor_tensor(keys[:, 0:BATCHES], group[:, 0:BATCHES], ids2[:, :], ALU.add))
                then(nc.vector.tensor_tensor(keys[:, BATCHES:], group[:, BATCHES:], id2, ALU.add))
                settled()
                key_row, key = keys[:, 0:BATCHES], keys[:, BATCHES:BATCHES + 1]
                then(nc.vector.tensor_scalar(less[:, :], numbers, num_col[:, 0:1], None, ALU.is_lt))
                then(nc.vector.tensor_scalar(more[:, :], key_row, key, None, ALU.is_gt))
                then(nc.vector.tensor_scalar(facts[:, 4:5], facts[:, 4:5], float(N_LORA0), None, ALU.add))
                then(nc.vector.tensor_tensor(low_mask[:, :], mask_p, mask_r, ALU.is_equal))
                settled()
                then(nc.vector.tensor_tensor(same[:, :], same[:, :], less[:, :], ALU.mult))
                settled()
                then(nc.vector.tensor_scalar(less[:, :], key_row, key, None, ALU.is_lt))
                then(nc.vector.tensor_reduce(counts[:, 0:1], same[:, :], AX.X, ALU.add))
                settled()
                then(nc.vector.tensor_reduce(counts[:, 1:2], less[:, :], AX.X, ALU.add))
                then(nc.vector.tensor_scalar(counts[:, 3:4], counts[:, 0:1], 0.0, None, ALU.is_equal))
                settled()
                then(nc.vector.tensor_tensor(counts[:, 2:3], counts[:, 0:1], counts[:, 1:2], ALU.add))
                settled()
                then(nc.vector.tensor_scalar(one_hot[:, :], num_row[:, :], counts[:, 2:3], None, ALU.is_equal))
                then(nc.vector.tensor_scalar(counts[:, 1:2], id2, 1.0, counts[:, 3:4], ALU.add, ALU.mult))
                dve.wait_ge(order_mm, 2)
                then(nc.vector.tensor_copy(facts[:, 5:6], tab_ps[0:BATCHES, BANK - 1:BANK]))
                settled()
                then(nc.vector.tensor_scalar(rank_hot[:, :], num_row[:, 0:MATS2 + 1], facts[:, 5:6], None, ALU.is_equal))
                dve.wait_ge(order_mm, 3)
                then(nc.vector.tensor_copy(table[:, 0:T_FACTS], tab_ps[0:1, 0:T_FACTS]))
                settled()
                ranks = table[:, T_RANK:T_RANK + BATCHES].rearrange("o (j s) -> o s j", s=2)
                nc.vector.tensor_tensor(table[:, T_MIXED:T_ALL], ranks[:, 1, :], ranks[:, 0, :],
                                        ALU.subtract).then_inc(table_ready, 1)
                assert steps[0] == ORDER_STEPS + 1

            def convert(turn, h, half_at):
                for k in range(h * HK, (h + 1) * HK):
                    dve.wait_ge(w_hi, turn * KT + (k + 1))
                    split = w_ring[:, half_at, k % HK]
                    nc.vector.tensor_tensor(split[:, 1, :], w_stage[:, k % STAGES, :], split[:, 0, :],
                                            ALU.subtract).then_inc(w_lo, 1)

            def x_lo(s, p, h, lora):
                dve.wait_ge(x_hi_ready, 2 * s + (h + 1))
                nc.vector.tensor_tensor(xs_of(h, 1), x_of(p, h), xs_of(h, 0), ALU.subtract).then_inc(x_lo_ready, 1)
                if lora:
                    dve.wait_ge(a_hi_ready, 2 * s + (h + 1))
                    for b in range(2):
                        split = a_split_of(h, b)
                        op = nc.vector.tensor_tensor(split[:, :, GROUPS - 1, :], a_of(h, b), split[:, :, 0, :],
                                                     ALU.subtract)
                    op.then_inc(a_lo_ready, 1)

            def low(t, parity):
                dve.wait_ge(quarters, 4 * t + 4)
                dve.wait_ge(y_done, t + 1)
                dve.wait_ge(b_lo, t + 1)
                nc.vector.tensor_tensor(low_a[:, :], low_ps[0:KL, parity, P:2 * P], low_scale[:, :], ALU.mult).then_inc(low_step, 1)
                nc.vector.tensor_tensor(low_sum[:, :], low_ps[0:KL, parity, 0:P], low_scale[:, :], ALU.mult).then_inc(low_step, 1)
                dve.wait_ge(low_step, 4 * t + 2)
                nc.vector.tensor_tensor(low_sum[:, :], low_sum[:, :], low_a[:, :], ALU.add).then_inc(low_step, 1)
                dve.wait_ge(low_step, 4 * t + 3)
                nc.vector.tensor_copy(low_split[:, :], low_sum[:, :]).then_inc(low_step, 1)
                dve.wait_ge(low_step, 4 * t + 4)
                third = slice(2 * GROUP, 3 * GROUP)
                nc.vector.tensor_tensor(low_split[third, :], low_sum[third, :], low_split[third, :],
                                        ALU.subtract).then_inc(low_ready, 1)

            def b_lo_part(t):
                dve.wait_ge(b_hi, t + 1)
                second = slice(GROUP, 2 * GROUP)
                nc.vector.tensor_tensor(b_split[second, :], b_stage[second, 0:FEATS], b_split[second, :], ALU.subtract)
                nc.vector.tensor_scalar(low_scale[:, :], low_mask[:, :], b_stage[:, FEATS:FEATS + 1], None,
                                        ALU.mult).then_inc(b_lo, 1)

            def update_x(t, p, layer):
                dve.wait_ge(t_done, t + 3)
                for k in range(KT):
                    x = x_all[:, p, :, k, :]
                    op = nc.vector.scalar_tensor_tensor(
                        out=x, in0=t_ps[:, k * P:(k + 1) * P].rearrange("p (b r) -> p b r", b=2),
                        scalar=bias_sb[:, layer, k:k + 1], in1=x, op0=ALU.add, op1=ALU.add)
                op.then_inc(x_updated, 1)

            def lora_step(t, parity, p, layer, first=False, updated=None, turn=None, lora=True):
                if not first:
                    low(t - 1, 1 - parity)
                if updated:
                    update_x(t - 2, *updated)
                if turn is not None:
                    convert(turn, 0, ring_half(turn, 0))
                b_lo_part(t)
                p_next = p + 1 if turn is None else 0
                x_lo(t + 1, p_next, 0, lora)
                if turn is not None:
                    convert(turn, 1, ring_half(turn, 1))
                x_lo(t + 1, p_next, 1, lora)

            dve.sem_inc(low_ready, 2)
            dve.sem_inc(x_updated, 1)
            dve.sem_inc(out_ready, 1)
            order_the_batches()
            convert(0, 0, 0)
            x_lo(0, 0, 0, True)
            convert(0, 1, 1)
            x_lo(0, 0, 1, True)
            dve.wait_ge(bias_in, 16)

            lora_step(0, 0, 0, 0, first=True)
            lora_step(1, 1, 1, 0)
            lora_step(2, 0, 2, 0, updated=(0, 0))
            with dve.Fori(1, PAIRS // 2 - 1) as i:
                t = 2 * i + 1
                lora_step(t, 1, t, 0, updated=(t - 2, 0))
                lora_step(t + 1, 0, t + 1, 0, updated=(t - 1, 0))
            lora_step(PAIRS - 1, 1, PAIRS - 1, 0, updated=(PAIRS - 3, 0), turn=1)
            lora_step(PAIRS, 0, 0, 1, updated=(PAIRS - 2, 0))
            lora_step(PAIRS + 1, 1, 1, 1, updated=(PAIRS - 1, 0))
            lora_step(PAIRS + 2, 0, 2, 1, updated=(0, 1))
            with dve.Fori(1, PAIRS // 2 - 1) as i:
                p = 2 * i + 1
                lora_step(p + PAIRS, 1, p, 1, updated=(p - 2, 1))
                lora_step(p + (PAIRS + 1), 0, p + 1, 1, updated=(p - 1, 1))
            lora_step(2 * PAIRS - 1, 1, PAIRS - 1, 1, updated=(PAIRS - 3, 1), turn=2, lora=False)

            def x3_lo_part(j, parity):
                dve.wait_ge(y_taken, j + (2 * PAIRS + 3))
                dve.wait_ge(l3_done, j + 1)
                nc.vector.tensor_tensor(x3_lo[:, :], rows[:, parity, :], x3_hi[:, :], ALU.subtract).then_inc(x3_split, 1)

            def finish_out(j, parity):
                dve.wait_ge(l3_done, j + 2)
                nc.vector.tensor_tensor(rows[:, parity, :], t_ps[:, :], rows[:, parity, :], ALU.add).then_inc(out_ready, 1)

            def switch_step(j, parity, first=False, last=False):
                if first:
                    low(2 * PAIRS - 1, 1)
                    update_x(2 * PAIRS - 2, PAIRS - 2, 1)
                else:
                    x3_lo_part(j - 1, 1 - parity)
                ra, rb = rank_of(dve, j, 0), rank_of(dve, j, 1)
                with dve.If(ra != rb):
                    convert(rb + 2, 0, ring_half(rb + 2, 0))
                    convert(rb + 2, 1, ring_half(rb + 2, 1))
                if not last:
                    rn = rank_of(dve, j, 2)
                    with dve.If(rn != rb):
                        convert(rn + 2, 0, ring_half(rn + 2, 0))
                if not first:
                    finish_out(j - 1, 1 - parity)
                dve.wait_ge(w3_hi_ready, j + 1)
                nc.vector.tensor_tensor(w3_lo[:, :], w3_stage[:, :], w3_hi[:, :], ALU.subtract).then_inc(w3_lo_ready, 1)
                if not last:
                    s = j + (2 * PAIRS + 1)
                    x_lo(s, j + 1, 0, False)
                    with dve.If(rn != rb):
                        convert(rn + 2, 1, ring_half(rn + 2, 1))
                    x_lo(s, j + 1, 1, False)

            switch_step(0, 0, first=True)
            update_x(2 * PAIRS - 1, PAIRS - 1, 1)
            with dve.Fori(0, PAIRS // 2 - 1) as i:
                switch_step(2 * i + 1, 1)
                switch_step(2 * i + 2, 0)
            switch_step(PAIRS - 1, 1, last=True)
            x3_lo_part(PAIRS - 1, 1)
            finish_out(PAIRS - 1, 1)

        @block.tensor
        def _(pe):
            def order_products():
                pe.wait_ge(iota_ready, 5)
                pe.wait_ge(order_step, ORDER_SAME)
                nc.tensor.matmul(tab_ps[0:BATCHES, 0:BATCHES], ones[:, :], same[:, :],
                                 start=True, stop=True).then_inc(order_mm, 1)
                pe.wait_ge(order_step, ORDER_RANK)
                nc.tensor.matmul(tab_ps[0:BATCHES, BANK - 1:BANK], more[:, :], counts[:, 3:4],
                                 start=True, stop=True).then_inc(order_mm, 1)
                pe.wait_ge(order_step, ORDER_STEPS)
                for fact, at, n in ((0, T_BATCH, SLOTS), (1, T_COND, SLOTS), (2, T_MAT, SLOTS), (5, T_RANK, SLOTS),
                                    (3, T_LORA, BATCHES), (4, T_LORA + BATCHES, BATCHES)):
                    nc.tensor.matmul(tab_ps[0:1, at:at + n], facts[:, fact:fact + 1], one_hot[:, 0:n],
                                     start=True, stop=True)
                op = nc.tensor.matmul(tab_ps[0:1, T_USED:T_FACTS], counts[:, 1:2], rank_hot[:, :],
                                      start=True, stop=True)
                op.then_inc(order_mm, 1)

            def half(h, parity, half_at, m=P, lora=None, stop=True, each_tile=None, marks=()):
                for k in range(h * HK, (h + 1) * HK):
                    if each_tile is not None:
                        pe.wait_ge(w_lo, each_tile + k + 1)
                    for part_x, part_w in ((0, 0), (0, 1), (1, 0)):
                        for n in range(NB):
                            cols = slice(n * BANK, (n + 1) * BANK)
                            op = nc.tensor.matmul(
                                y_ps[0:m, parity, cols], xs[:, k, part_x, 0:m], w_ring[:, half_at, k % HK, part_w, cols],
                                start=k == 0 and part_x == part_w, stop=stop and k == KT - 1 and part_x == 1)
                    if lora is not None:
                        if k == h * HK:
                            pe.wait_ge(a_hi_ready, 2 * lora + (h + 1))
                            pe.wait_ge(a_lo_ready, 2 * lora + (h + 1))
                        op = nc.tensor.matmul(low_ps[0:KL, parity, 0:2 * P], a_split[:, k, :],
                                              xs[:, k].rearrange("p s r -> p (s r)"), start=k == 0, stop=k == KT - 1)
                    if k in marks:
                        op.then_inc(quarters, 1)

            def lora_b(t, parity):
                pe.wait_ge(low_ready, t + 3)
                pe.wait_ge(b_lo, t + 1)
                for n in range(NB):
                    cols = slice(n * BANK, (n + 1) * BANK)
                    op = nc.tensor.matmul(y_ps[:, parity, cols], low_split[:, :], b_split[:, cols], start=False, stop=True)
                op.then_inc(y_done, 1)

            def transposes(t, parity):
                pe.wait_ge(y_taken, t + 3)
                pe.wait_ge(x_updated, t + 1)
                for k in range(KT):
                    cols = slice(k * P, (k + 1) * P)
                    op = nc.tensor.transpose(t_ps[:, cols], rows[:, parity, cols], ident[:, :])
                op.then_inc(t_done, 1)

            def operands(s, h):
                pe.wait_ge(x_hi_ready, 2 * s + (h + 1))
                pe.wait_ge(x_lo_ready, 2 * s + (h + 1))

            MARKS = (HK - 3, HK - 2, HK - 1, KT - 1)

            def lora_step(t, parity, turn, first=False):
                pe.wait_ge(y_taken, t + 1)
                pe.wait_ge(low_ready, t + 1)
                operands(t, 0)
                pe.wait_ge(w_lo, turn * KT + (1 if first else HK))
                half(0, parity, ring_half(turn, 0), lora=t, stop=False, each_tile=turn * KT if first else None, marks=MARKS)
                if not first:
                    lora_b(t - 1, 1 - parity)
                operands(t, 1)
                if not first:
                    pe.wait_ge(w_lo, turn * KT + KT)
                half(1, parity, ring_half(turn, 1), lora=t, stop=False, each_tile=turn * KT if first else None, marks=MARKS)
                if not first:
                    transposes(t - 1, 1 - parity)

            pe.sem_inc(y_done, 1)
            pe.sem_inc(t_done, 2)
            pe.sem_inc(l3_done, 1)
            order_products()
            pe.wait_ge(ident_ready, 1)
            for layer in range(2):
                s = layer * PAIRS
                lora_step(s, 0, layer, first=layer == 0)
                with pe.Fori(0, PAIRS // 2 - 1) as i:
                    lora_step(2 * i + (s + 1), 1, layer)
                    lora_step(2 * i + (s + 2), 0, layer)
                lora_step(s + PAIRS - 1, 1, layer)

            def layer3(j, parity):
                pe.wait_ge(x3_split, j + 1)
                pe.wait_ge(w3_lo_ready, j + 1)
                pe.wait_ge(x_updated, 2 * PAIRS + 1)
                pe.wait_ge(out_ready, j + 1)
                for w, x in ((w3_hi, x3_hi), (w3_hi, x3_lo), (w3_lo, x3_hi)):
                    for n in range(NB):
                        cols = slice(n * BANK, (n + 1) * BANK)
                        op = nc.tensor.matmul(t_ps[:, cols], w[:, :], x[:, cols],
                                              start=w is w3_hi and x is x3_hi, stop=w is w3_lo)
                op.then_inc(l3_done, 1)

            def switch_step(j, parity, first=False):
                s = j + 2 * PAIRS
                ra, rb = rank_of(pe, j, 0), rank_of(pe, j, 1)
                pe.wait_ge(y_taken, s + 1)
                operands(s, 0)
                pe.wait_ge(w_lo, ra * KT + (2 * KT + HK))
                a_half, b_half = (tuple(ring_half(r + 2, h) for h in range(2)) for r in (ra, rb))
                with pe.If(ra != rb):
                    half(0, parity, a_half[0], marks=(HK - 1,))
                with pe.Else():
                    half(0, parity, a_half[0], marks=MARKS)
                if first:
                    lora_b(2 * PAIRS - 1, 1)
                else:
                    layer3(j - 1, 1 - parity)
                operands(s, 1)
                pe.wait_ge(w_lo, ra * KT + (2 * KT + KT))
                with pe.If(ra != rb):
                    half(1, parity, a_half[1], marks=(KT - 1,))
                    pe.wait_ge(w_lo, rb * KT + (2 * KT + HK))
                    half(0, parity, b_half[0], m=ROWS, marks=(HK - 1,))
                    pe.wait_ge(w_lo, rb * KT + (2 * KT + KT))
                    half(1, parity, b_half[1], m=ROWS, marks=(KT - 1,))
                with pe.Else():
                    half(1, parity, a_half[1], marks=MARKS)
                if first:
                    transposes(2 * PAIRS - 1, 1)

            pe.wait_ge(table_ready, 1)
            switch_step(0, 0, first=True)
            with pe.Fori(0, PAIRS // 2 - 1) as i:
                switch_step(2 * i + 1, 1)
                switch_step(2 * i + 2, 0)
            switch_step(PAIRS - 1, 1)
            layer3(PAIRS - 1, 1)


def kernel(x, itok_B_1_7, itok_B_6_15, itok_B_3_7, itok_B_0_15, L0_cond_weight, L0_cond_bias,
           L0_cond_lora_a_weights, L0_cond_lora_b_weights, L0_cond_scaling_factors, L1_cond_base_weight,
           L1_cond_base_bias, L1_cond_lora_A_w, L1_cond_lora_B_w, L2_cond_weight, L3_cond_weights):
    import numpy as np
    import concourse.bacc as bacc
    from concourse.bass_utils import run_bass_kernel_spmd

    def arr(a):
        return np.asarray(a)

    def a_layout(a):
        n = a.shape[0]
        return arr(a).reshape(n, RANK, KT, P).transpose(0, 3, 2, 1).reshape(n, P, KT * RANK)

    def b_layout(b, scale):
        n = b.shape[0]
        scale = np.broadcast_to(arr(scale)[:, None, None], (n, RANK, 1))
        return np.concatenate([arr(b).transpose(0, 2, 1), scale], axis=2)

    ids = np.stack([arr(i) for i in (itok_B_0_15, itok_B_3_7, itok_B_1_7, itok_B_6_15)], axis=1)
    weights = np.concatenate([arr(L0_cond_weight)[None], arr(L1_cond_base_weight)[None], arr(L2_cond_weight)])
    ones = np.ones(L1_cond_lora_A_w.shape[0], np.float32)
    arrays = {
        "xt": arr(x).reshape(BATCHES, ROWS, KT, P).transpose(0, 3, 2, 1).reshape(BATCHES, P, KT * ROWS),
        "ids_cols": ids.astype(np.int32),
        "ids2_row": arr(itok_B_3_7).reshape(1, BATCHES).astype(np.int32),
        "wt": weights.transpose(0, 2, 1).reshape(2 + MATS2, KT, P, FEATS),
        "bias": np.stack([arr(L0_cond_bias), arr(L1_cond_base_bias)]).reshape(2, KT, P).transpose(2, 0, 1),
        "a_tab": np.concatenate([a_layout(L0_cond_lora_a_weights), a_layout(L1_cond_lora_A_w)]),
        "b_tab": np.concatenate([b_layout(L0_cond_lora_b_weights, L0_cond_scaling_factors),
                                 b_layout(L1_cond_lora_B_w, ones)]),
        "w3": arr(L3_cond_weights),
    }
    arrays = {name: np.ascontiguousarray(a) for name, a in arrays.items()}
    nc = bacc.Bacc("TRN2", target_bir_lowering=False, num_devices=1, dynamic_dma_scratch_size=1024)
    args = {name: nc.dram_tensor(name, a.shape, mybir.dt.from_np(a.dtype), kind="ExternalInput").ap()
            for name, a in arrays.items()}
    out = nc.dram_tensor("out", (BATCHES, ROWS, FEATS), F32, kind="ExternalOutput").ap()
    build(nc, out=out, **args)
    return run_bass_kernel_spmd(nc, [arrays], core_ids=[0]).results[0]["out"]
```

```python
from contextlib import ExitStack

import concourse.bass as bass
from concourse import mybir

F32 = mybir.dt.float32
F32R = mybir.dt.float32r
I32 = mybir.dt.int32
ALU = mybir.AluOpType
AX = mybir.AxisListType

P = 128
BATCHES, ROWS, FEATS = 32, 64, 1024
PAIRS = BATCHES // 2
KT = FEATS // P
HK = KT // 2
RANK = 16
MATS2 = 8
N_LORA0 = 8
BANK = 512
NB = FEATS // BANK
GROUPS = 4
B_LO, LOW_LO = 1, 2
KL = 2 * GROUPS * RANK
STAGES = 4

SLOTS = BATCHES + 2
T_BATCH = 0
T_LORA = T_BATCH + SLOTS
T_COND = T_LORA + 2 * BATCHES
T_RANK = T_COND + SLOTS
T_USED = T_RANK + SLOTS
T_FACTS = T_USED + MATS2 + 1
T_MIXED, T_FOLLOWING, T_START = (T_FACTS + n * PAIRS for n in range(3))
T_ALL = T_START + PAIRS
SLOT_OF = (1, 0)
WARM_UPS = 9
AHEAD = STAGES
LANDED = 16 * KT // STAGES
MASK_STEPS = 7
ORDER_SAME, ORDER_PLACES, ORDER_FIRSTS, ORDER_STEPS = 3, 16, 18, 21


def build(nc, xt, ids_cols, ids2_row, wt, bias, a_tab, b_tab, w3, out):
    ctx = ExitStack()
    with ctx:
        def sb(name, shape, dt):
            return ctx.enter_context(nc.sbuf_tensor(name, shape, dt))

        def psum(name, shape):
            return ctx.enter_context(nc.psum_tensor(name, shape, F32))

        def sem(name):
            return ctx.enter_context(nc.semaphore(name))

        x_all = sb("x_all", [P, PAIRS, 2, KT, ROWS], F32)
        w_ring = sb("w_ring", [P, 3, HK, 2, FEATS], F32R)
        w_stage = sb("w_stage", [P, STAGES, FEATS], F32)
        xs = sb("xs", [P, KT, 2, P], F32R)
        a_stage = sb("a_stage", [P, 2, KT, RANK], F32)
        a_split = sb("a_split", [P, KT, KL], F32R)
        b_stage = sb("b_stage", [KL, FEATS + 1], F32)
        b_split = sb("b_split", [KL, FEATS], F32R)
        low_mask = sb("low_mask", [KL, P], F32)
        group_of = sb("group_of", [KL, 1], I32)
        b_is_lo, b_sign = sb("b_is_lo", [KL, 1], F32), sb("b_sign", [KL, 1], F32)
        low_is_lo, low_sign = sb("low_is_lo", [KL, 1], F32), sb("low_sign", [KL, 1], F32)
        low_scale = sb("low_scale", [KL, P], F32)
        low_a = sb("low_a", [KL, P], F32)
        low_sum = sb("low_sum", [KL, P], F32)
        low_split = sb("low_split", [KL, P], F32R)
        rows = sb("rows", [P, 2, FEATS], F32)
        x3_hi = sb("x3_hi", [P, FEATS], F32R)
        x3_lo = sb("x3_lo", [P, FEATS], F32R)
        w3_stage = sb("w3_stage", [P, P], F32)
        w3_hi = sb("w3_hi", [P, P], F32R)
        w3_lo = sb("w3_lo", [P, P], F32R)
        bias_sb = sb("bias_sb", [P, 2, KT], F32)
        ident = sb("ident", [P, P], F32)
        B = BATCHES
        ids_i = sb("ids_i", [B, 4], I32)
        ids2_i = sb("ids2_i", [B, B], I32)
        ids2 = sb("ids2", [B, B + 1], F32)
        num_col = sb("num_col", [B, 1], F32)
        num_row = sb("num_row", [B, SLOTS], F32)
        group = sb("group", [B, B + 1], I32)
        keys = sb("keys", [B, B + 1], F32)
        ones = sb("ones", [B, B], F32)
        same = sb("same", [B, B], F32)
        less = sb("less", [B, B], F32)
        more = sb("more", [B, B], F32)
        counts = sb("counts", [B, 4], F32)
        one_hot = sb("one_hot", [B, SLOTS], F32)
        rank_hot = sb("rank_hot", [B, MATS2 + 1], F32)
        facts = sb("facts", [B, 6], F32)
        table = sb("table", [1, T_ALL], I32)
        rank_step = sb("rank_step", [1, PAIRS], I32)
        ranks_left = sb("ranks_left", [1, PAIRS], I32)

        y_ps = psum("y_ps", [P, 2, FEATS])
        t_ps = psum("t_ps", [P, FEATS])
        low_ps = psum("low_ps", [P, 2, BANK])
        sums_ps, table_ps = low_ps[:, 1, :], t_ps[0:1, :]
        LORA_COL = BANK

        ids_in, bias_in = sem("ids_in"), sem("bias_in")
        x_in = [sem(f"x_in{n}") for n in range(2)]
        w_in = [sem(f"w_in{n}") for n in range(STAGES)]
        a_in, b_in, w3_in = sem("a_in"), sem("b_in"), sem("w3_in")
        stored = [sem(f"stored{n}") for n in range(2)]
        iota_ready, zeros_ready, ident_zero, ident_ready = (
            sem("iota_ready"), sem("zeros_ready"), sem("ident_zero"), sem("ident_ready"))
        order_step, order_mm = sem("order_step"), sem("order_mm")
        batches_ready, loras_ready, table_ready = sem("batches_ready"), sem("loras_ready"), sem("table_ready")
        mask_step, steps_one, plan_step, plan_ready = (
            sem("mask_step"), sem("steps_one"), sem("plan_step"), sem("plan_ready"))
        w_folded, w_hi, w_lo = sem("w_folded"), sem("w_hi"), sem("w_lo")
        w3_folded, w3_hi_ready, w3_lo_ready = sem("w3_folded"), sem("w3_hi_ready"), sem("w3_lo_ready")
        x_hi_ready, x_lo_ready = sem("x_hi_ready"), sem("x_lo_ready")
        a_hi_ready, a_lo_ready = sem("a_hi_ready"), sem("a_lo_ready")
        quarters = sem("quarters")
        low_step, low_ready = sem("low_step"), sem("low_ready")
        b_hi, b_lo = sem("b_hi"), sem("b_lo")
        y_done, y_taken = sem("y_done"), sem("y_taken")
        t_done, x_updated = sem("t_done"), sem("x_updated")
        x3_hi_ready = sem("x3_hi_ready")
        l3_done, out_ready = sem("l3_done"), sem("out_ready")

        def entry(eng, at, most):
            return eng.value_load(table[0:1, bass.ds(at, 1)], min_val=0, max_val=most)

        def first_rank(eng, j):
            return entry(eng, 2 * j + T_RANK, MATS2 - 1)

        def plan(eng, j):
            return (entry(eng, j + at, 1) for at in (T_MIXED, T_FOLLOWING, T_START))

        def ring_half(turn, h):
            return (2 * turn + h) % 3

        FIRST_HALF, SECOND_HALF = range(HK), range(HK, KT)
        FIRST_QUARTERS = (range(HK // 2), range(HK // 2, HK))
        BANKS = [slice(n * BANK, (n + 1) * BANK) for n in range(NB)]

        block = ctx.enter_context(nc.Block())

        @block.sync
        def _(sp):
            def load_chunk(matrix, k, turn):
                if not (isinstance(turn, int) and turn == 0 and k < STAGES):
                    sp.wait_ge(w_hi, turn * KT + (k - STAGES + 1))
                    sp.wait_ge(w_lo, turn * KT + (k - STAGES + 1))
                sp.dma_start(w_stage[:, k % STAGES, :], wt[matrix, k]).then_inc(w_in[k % STAGES], 16)

            def of_pair(start, at, most):
                return [entry(sp, at + (start + slot), most) for slot in SLOT_OF]

            def loras(t):
                return of_pair(T_LORA, 2 * t, a_tab.shape[0] - 1)

            def load_x(batches, p, parity):
                for b in range(2):
                    sp.dma_start(x_all[:, p, b].rearrange("p k r -> p (k r)"), xt[batches[b]]).then_inc(x_in[parity], 16)

            def load_a(which):
                for b in range(2):
                    sp.dma_start(a_stage[:, b].rearrange("p k r -> p (k r)"), a_tab[which[b]]).then_inc(a_in, 16)

            def load_b(which):
                for b in range(2):
                    rows_of_b = b_stage[b * GROUPS * RANK:(b + 1) * GROUPS * RANK, :]
                    sp.dma_start(rows_of_b, b_tab[which[b]].unsqueeze(0).to_broadcast(
                        [GROUPS, RANK, FEATS + 1])).then_inc(b_in, 16)

            def load_w3(conds):
                for b in range(2):
                    r = slice(b * ROWS, (b + 1) * ROWS)
                    sp.dma_start(w3_stage[r, r], w3[conds[b]]).then_inc(w3_in, 16)

            def lora_step(t, parity, p=None, chunks=(), b_of=None):
                which = loras(t + 1)
                batches = None if p is None else of_pair(T_BATCH, 2 * p, BATCHES - 1)
                sp.wait_ge(a_hi_ready, 2 * t + 2)
                sp.wait_ge(a_lo_ready, 2 * t + 2)
                load_a(which)
                if p is not None:
                    if parity == 1:
                        sp.wait_ge(x_in[0], 16 * p)
                    elif not isinstance(p, int):
                        sp.wait_ge(x_in[1], 16 * p - 16)
                    load_x(batches, p, 1 - parity)
                if b_of:
                    load_b(b_of)
                for chunk in chunks:
                    load_chunk(*chunk)
                sp.wait_ge(b_hi, t + 1)
                sp.wait_ge(b_lo, t + 1)
                load_b(which)

            for n in range(2):
                sp.sem_inc(stored[n], 16)
            sp.dma_start(ids_i[:, :], ids_cols).then_inc(ids_in, 16)
            sp.dma_start(ids2_i[:, :], ids2_row.to_broadcast([BATCHES, BATCHES])).then_inc(ids_in, 16)
            for k in range(AHEAD):
                load_chunk(0, k, 0)
            sp.dma_start(bias_sb[:, :, :], bias).then_inc(bias_in, 16)
            sp.wait_ge(batches_ready, 1)
            for b in range(2):
                batch = entry(sp, T_BATCH + SLOT_OF[b], BATCHES - 1)
                sp.dma_start(x_all[:, 0, b].rearrange("p k r -> p (k r)"), xt[batch]).then_inc(x_in[0], 16)
            sp.wait_ge(loras_ready, 1)
            which = loras(0)
            load_a(which)
            for k in range(AHEAD, KT):
                load_chunk(0, k, 0)

            lora_step(0, 0, p=1, b_of=which)
            lora_step(1, 1, p=2, chunks=[(1, k, 1) for k in FIRST_QUARTERS[0]])
            lora_step(2, 0, p=3, chunks=[(1, k, 1) for k in FIRST_QUARTERS[1]])
            with sp.Fori(1, PAIRS // 2 - 1) as i:
                lora_step(2 * i + 1, 1, p=2 * i + 2)
                lora_step(2 * i + 2, 0, p=2 * i + 3)
            for k in range(STAGES, KT):
                load_chunk(1, k, 1)
            lora_step(PAIRS - 1, 1)

            def first_chunks(rank):
                used = entry(sp, rank + T_USED, MATS2)
                with sp.If(used != 0):
                    for k in range(STAGES):
                        load_chunk(used + 1, k, rank + 2)

            def other_chunks(rank):
                used = entry(sp, rank + T_USED, MATS2)
                for k in range(STAGES, KT):
                    load_chunk(used + 1, k, rank + 2)

            sp.wait_ge(table_ready, 1)
            matrix = entry(sp, T_USED, MATS2) + 1
            lora_step(PAIRS, 0, chunks=[(matrix, k, 2) for k in range(STAGES)])
            with sp.Fori(0, PAIRS // 2 - 1) as i:
                lora_step(2 * i + (PAIRS + 1), 1)
                lora_step(2 * i + (PAIRS + 2), 0)
            sp.wait_ge(zeros_ready, 1)
            load_w3(of_pair(T_COND, 0, w3.shape[0] - 1))
            other_chunks(0)
            first_chunks(1)

            def store(batches, j, parity):
                sp.wait_ge(out_ready, j + 2)
                for b in range(2):
                    sp.dma_start(out[batches[b]], rows[b * ROWS:(b + 1) * ROWS, parity, :]).then_inc(stored[parity], 16)

            def switch_step(j, parity, first=False, last=False, storing=True):
                rank = first_rank(sp, j)
                mixed, following, start = plan(sp, j)
                batches = of_pair(T_BATCH, 2 * j - 4, BATCHES - 1) if storing else None
                conds = None if first else of_pair(T_COND, 2 * j, w3.shape[0] - 1)
                if storing:
                    store(batches, j - 2, parity)
                if not first:
                    sp.wait_ge(w3_hi_ready, j)
                    sp.wait_ge(w3_lo_ready, j)
                    load_w3(conds)
                with sp.If(start != 0):
                    other_chunks(rank + 1)
                with sp.If(mixed != 0):
                    first_chunks(rank + 2)
                    if not last:
                        with sp.If(following != 0):
                            other_chunks(rank + 2)
                if not last:
                    with sp.If(following != 0):
                        first_chunks(rank + mixed + 2)

            sp.wait_ge(plan_ready, 1)
            switch_step(0, 0, first=True, storing=False)
            switch_step(1, 1, storing=False)
            switch_step(2, 0)
            with sp.Fori(1, PAIRS // 2 - 1) as i:
                switch_step(2 * i + 1, 1)
                switch_step(2 * i + 2, 0)
            switch_step(PAIRS - 1, 1, last=True)
            store(of_pair(T_BATCH, BATCHES - 4, BATCHES - 1), PAIRS - 2, 0)
            batches = of_pair(T_BATCH, BATCHES - 2, BATCHES - 1)
            for n in range(NB):
                sp.wait_ge(out_ready, PAIRS + 1 + n)
                cols = slice(n * BANK, (n + 1) * BANK)
                for b in range(2):
                    sp.dma_start(out[batches[b]][:, cols], rows[b * ROWS:(b + 1) * ROWS, 1, cols]).then_inc(stored[1], 16)
            sp.wait_ge(stored[0], 16 + 16 * PAIRS)
            sp.wait_ge(stored[1], 16 + 16 * PAIRS + 16 * 2 * (NB - 1))

        @block.gpsimd
        def _(pool):
            nc.gpsimd.iota(num_col[:, :], pattern=[[0, 1]], base=0, channel_multiplier=1,
                           allow_small_or_imprecise_dtypes=True).then_inc(iota_ready, 1)
            nc.gpsimd.iota(num_row[:, :], pattern=[[1, SLOTS]], base=0, channel_multiplier=0,
                           allow_small_or_imprecise_dtypes=True).then_inc(iota_ready, 1)
            nc.gpsimd.iota(low_a[:, :].bitcast(I32), pattern=[[0, P]], base=0, channel_multiplier=1).then_inc(iota_ready, 1)
            nc.gpsimd.iota(low_sum[:, :].bitcast(I32), pattern=[[1, 2], [0, ROWS]], base=0, channel_multiplier=0).then_inc(iota_ready, 1)
            nc.gpsimd.memset(ones[:, :], 1.0).then_inc(iota_ready, 1)
            nc.gpsimd.memset(rank_step[:, :], 1).then_inc(steps_one, 1)
            nc.gpsimd.memset(w3_stage[:, :], 0.0).then_inc(zeros_ready, 1)
            nc.gpsimd.memset(ident[:, :], 0.0).then_inc(ident_zero, 1)
            pool.wait_ge(ident_zero, 1)
            nc.gpsimd.affine_select(out=ident[:, :], in_=ident[:, :], compare_op=ALU.not_equal, fill=1.0,
                                    base=0, pattern=[[-1, P]], channel_multiplier=1).then_inc(ident_ready, 1)
            pool.wait_ge(ident_ready, 1)

            def fold(r, tiles):
                for k in tiles:
                    pool.wait_ge(w_in[k % STAGES], r * LANDED + (2 * LANDED + 16 * (k // STAGES + 1)))
                    diag = w_stage[:, k % STAGES, k * P:(k + 1) * P]
                    nc.gpsimd.tensor_tensor(diag, diag, ident[:, :], ALU.add).then_inc(w_folded, 1)

            fold(0, FIRST_HALF)
            fold(0, SECOND_HALF)
            pool.wait_ge(plan_ready, 1)
            with pool.Fori(0, PAIRS) as j:
                rank = first_rank(pool, j)
                mixed, following, start = plan(pool, j)
                with pool.If(start != 0):
                    fold(rank + 1, FIRST_HALF)
                with pool.If(mixed != 0):
                    fold(rank + 1, SECOND_HALF)
                    with pool.If(following != 0):
                        fold(rank + 2, FIRST_HALF)
                with pool.If(following != 0):
                    fold(rank + mixed + 1, SECOND_HALF)
                pool.wait_ge(w3_in, 32 * j + 32)
                nc.gpsimd.tensor_tensor(w3_stage[:, :], w3_stage[:, :], ident[:, :], ALU.add).then_inc(w3_folded, 1)

        def x_of(p, h):
            return x_all[:, p, :, h * HK:(h + 1) * HK, :].rearrange("p b k r -> p k b r")

        def xs_of(h, part):
            return xs[:, h * HK:(h + 1) * HK, part, :].rearrange("p k (b r) -> p k b r", b=2)

        def a_of(h, b):
            return a_stage[:, b, h * HK:(h + 1) * HK, :]

        def a_split_of(h, b):
            a = a_split[:, h * HK:(h + 1) * HK, :].rearrange("p k (b e r) -> p k b e r", e=GROUPS, b=2)
            return a[:, :, b, :, :]

        @block.scalar
        def _(act):
            def convert(turn, tiles, rank=None):
                for k in tiles:
                    half_at = ring_half(turn, k // HK)
                    if rank is None:
                        act.wait_ge(w_in[k % STAGES], turn * LANDED + 16 * (k // STAGES + 1))
                    else:
                        act.wait_ge(w_folded, rank * KT + (k + 1))
                    nc.scalar.copy(w_ring[:, half_at, k % HK, 0, :], w_stage[:, k % STAGES, :]).then_inc(w_hi, 1)

            def x_hi(s, p, h, lora):
                nc.scalar.copy(xs_of(h, 0), x_of(p, h)).then_inc(x_hi_ready, 1)
                if lora:
                    act.wait_ge(a_in, 32 * s + 32)
                    for b in range(2):
                        op = nc.scalar.copy(a_split_of(h, b)[:, :, 0:GROUPS - 1, :],
                                            a_of(h, b).unsqueeze(2).to_broadcast([P, HK, GROUPS - 1, RANK]))
                    op.then_inc(a_hi_ready, 1)

            def wait_x(s, parity, layer0):
                if layer0:
                    act.wait_ge(x_in[parity], 16 * s + (32 if parity == 0 else 16))
                else:
                    act.wait_ge(x_updated, s - (PAIRS - 2))

            def take_y(t, parity):
                act.wait_ge(y_done, t + 2)
                act.wait_ge(t_done, t + 1)
                nc.scalar.copy(rows[:, parity, :], y_ps[:, parity, :]).then_inc(y_taken, 1)

            def lora_step(t, parity, p_next, first=False, ahead=None, following=None, layer0=False, lora=True):
                def b_hi_part():
                    act.wait_ge(y_done, t + 1)
                    act.wait_ge(b_in, 32 * t + 32)
                    nc.scalar.mul(b_split[:, :], b_stage[:, 0:FEATS], b_sign[:, 0:1]).then_inc(b_hi, 1)

                if not first:
                    take_y(t - 1, 1 - parity)
                    b_hi_part()
                wait_x(t + 1, 1 - parity, layer0)
                act.wait_ge(quarters, 4 * t + 3)
                x_hi(t + 1, p_next, 0, lora)
                if first:
                    b_hi_part()
                if following:
                    turn, rank = following
                    convert(turn, SECOND_HALF, rank)
                act.wait_ge(quarters, 4 * t + 4)
                x_hi(t + 1, p_next, 1, lora)
                if ahead:
                    convert(*ahead)

            act.sem_inc(y_taken, 2)
            act.wait_ge(mask_step, MASK_STEPS)
            convert(0, range(AHEAD))
            wait_x(0, 0, True)
            x_hi(0, 0, 0, True)
            x_hi(0, 0, 1, True)
            convert(0, range(AHEAD, KT))

            early, late = FIRST_QUARTERS
            lora_step(0, 0, 1, first=True, layer0=True)
            lora_step(1, 1, 2, layer0=True)
            lora_step(2, 0, 3, layer0=True, ahead=(1, early))
            lora_step(3, 1, 4, layer0=True, ahead=(1, late))
            lora_step(4, 0, 5, layer0=True)
            with act.Fori(2, PAIRS // 2 - 1) as i:
                lora_step(2 * i + 1, 1, 2 * i + 2, layer0=True)
                lora_step(2 * i + 2, 0, 2 * i + 3, layer0=True)
            lora_step(PAIRS - 1, 1, 0, following=(1, None))

            lora_step(PAIRS, 0, 1)
            lora_step(PAIRS + 1, 1, 2, ahead=(2, early, 0))
            lora_step(PAIRS + 2, 0, 3, ahead=(2, late, 0))
            with act.Fori(1, PAIRS // 2 - 1) as i:
                lora_step(2 * i + (PAIRS + 1), 1, 2 * i + 2)
                lora_step(2 * i + (PAIRS + 2), 0, 2 * i + 3)
            act.wait_ge(plan_ready, 1)
            at_first = (first_rank(act, 0), *plan(act, 0))
            lora_step(2 * PAIRS - 1, 1, 0, following=(2, 0), lora=False)

            WHOLE = (slice(0, FEATS),)

            def x3_hi_part(j, parity, banks=WHOLE):
                act.wait_ge(l3_done, j + 1)
                for n, cols in enumerate(banks):
                    act.wait_ge(quarters, 4 * j + (4 * 2 * PAIRS + 4 + n))
                    nc.scalar.copy(x3_hi[:, cols], y_ps[:, parity, cols]).then_inc(x3_hi_ready, 1)

            def take_out(j, parity, banks=WHOLE):
                act.wait_ge(stored[parity], 16 * j + (16 if parity == 0 else 0))
                for n, cols in enumerate(banks):
                    act.wait_ge(l3_done, j + 2 + n)
                    nc.scalar.copy(rows[:, parity, cols], t_ps[:, cols]).then_inc(out_ready, 1)

            def split_w3(j):
                act.wait_ge(w3_folded, j + 1)
                act.wait_ge(l3_done, j + 1)
                nc.scalar.copy(w3_hi[:, :], w3_stage[:, :]).then_inc(w3_hi_ready, 1)

            def switch_step(j, parity, first=False, last=False, finishing=True):
                s4 = 4 * j + 4 * 2 * PAIRS

                def rest_of_first_half():
                    with act.If(start != 0):
                        convert(rank + 3, FIRST_QUARTERS[1], rank + 1)

                if first:
                    rank, mixed, following, start = at_first
                    with act.If(start != 0):
                        convert(rank + 3, FIRST_QUARTERS[0], rank + 1)
                    take_y(2 * PAIRS - 1, 1)
                else:
                    x3_hi_part(j - 1, 1 - parity)
                    rank = first_rank(act, j)
                    mixed, following, start = plan(act, j)
                    split_w3(j - 1)
                    if finishing:
                        take_out(j - 2, parity)
                    with act.If(start != 0):
                        convert(rank + 3, FIRST_HALF, rank + 1)
                with act.If(mixed != 0):
                    if first:
                        rest_of_first_half()
                    act.wait_ge(quarters, s4 + 1)
                    convert(rank + 3, SECOND_HALF, rank + 1)
                    if not last:
                        with act.If(following != 0):
                            act.wait_ge(quarters, s4 + 2)
                            convert(rank + 4, FIRST_HALF, rank + 2)
                if not last:
                    wait_x(j + (2 * PAIRS + 1), None, False)
                    act.wait_ge(quarters, s4 + 3)
                    x_hi(None, j + 1, 0, False)
                    if first:
                        with act.If(mixed == 0):
                            rest_of_first_half()
                    with act.If(following != 0):
                        convert(rank + mixed + 3, SECOND_HALF, rank + mixed + 1)
                    act.wait_ge(quarters, s4 + 4)
                    x_hi(None, j + 1, 1, False)

            switch_step(0, 0, first=True, finishing=False)
            switch_step(1, 1, finishing=False)
            switch_step(2, 0)
            with act.Fori(1, PAIRS // 2 - 1) as i:
                switch_step(2 * i + 1, 1)
                switch_step(2 * i + 2, 0)
            switch_step(PAIRS - 1, 1, last=True)
            take_out(PAIRS - 2, 0)
            split_w3(PAIRS - 1)
            x3_hi_part(PAIRS - 1, 1, BANKS)
            take_out(PAIRS - 1, 1, BANKS)

        @block.vector
        def _(dve):
            steps = [0]

            def then(op):
                op.then_inc(order_step, 1)
                steps[0] += 1

            def copy(to, what):
                then(nc.vector.tensor_copy(to, what))

            def settled():
                dve.wait_ge(order_step, steps[0])

            id2 = facts[:, 2:3]
            key_row, key = keys[:, 0:BATCHES], keys[:, BATCHES:BATCHES + 1]

            def masks():
                partition, batch_of_row = low_a[:, :].bitcast(I32), low_sum[:, :].bitcast(I32)
                log_rank, log_batch = RANK.bit_length() - 1, (GROUPS * RANK).bit_length() - 1
                dve.wait_ge(iota_ready, 4)
                nc.vector.tensor_scalar(group_of[:, :], partition[:, 0:1], log_rank, GROUPS - 1,
                                        ALU.logical_shift_right, ALU.bitwise_and).then_inc(mask_step, 1)
                dve.wait_ge(mask_step, 1)
                for is_lo, group in ((b_is_lo, B_LO), (low_is_lo, LOW_LO)):
                    nc.vector.tensor_scalar(is_lo[:, :], group_of[:, :], group, None, ALU.is_equal).then_inc(mask_step, 1)
                nc.vector.tensor_scalar(partition, partition, log_batch, None, ALU.logical_shift_right).then_inc(mask_step, 1)
                dve.wait_ge(mask_step, 4)
                for is_lo, sign in ((b_is_lo, b_sign), (low_is_lo, low_sign)):
                    nc.vector.tensor_scalar(sign[:, :], is_lo[:, :], -2.0, 1.0, ALU.mult, ALU.add).then_inc(mask_step, 1)
                nc.vector.tensor_tensor(low_mask[:, :], partition, batch_of_row, ALU.is_equal).then_inc(mask_step, 1)
                dve.wait_ge(mask_step, MASK_STEPS)

            def order_the_batches():
                dve.wait_ge(ids_in, 32)
                copy(facts[:, 1:5], ids_i[:, :])
                copy(ids2[:, 0:BATCHES], ids2_i[:, :])
                settled()
                then(nc.vector.tensor_scalar(same[:, :], ids2[:, 0:BATCHES], id2, None, ALU.is_equal))
                assert steps[0] == ORDER_SAME
                copy(ids2[:, BATCHES:], id2)
                dve.wait_ge(iota_ready, 4)
                then(nc.vector.tensor_scalar(num_row[:, :], num_row[:, :], float(BATCHES - 1), None, ALU.min))
                copy(facts[:, 0:1], num_col[:, :])
                settled()
                then(nc.vector.tensor_scalar(less[:, :], num_row[:, 0:BATCHES], num_col[:, 0:1], None, ALU.is_lt))
                dve.wait_ge(order_mm, 1)
                copy(group[:, :], sums_ps[0:BATCHES, 0:BATCHES + 1])
                settled()
                then(nc.vector.tensor_tensor(less[:, :], same[:, :], less[:, :], ALU.mult))
                settled()
                then(nc.vector.tensor_scalar(group[:, :], group[:, :], 1, MATS2.bit_length() - 1,
                                             ALU.bitwise_and, ALU.logical_shift_left))
                then(nc.vector.tensor_reduce(counts[:, 0:1], less[:, :], AX.X, ALU.add))
                settled()
                then(nc.vector.tensor_tensor(keys[:, :], group[:, :], ids2[:, :], ALU.add))
                settled()
                then(nc.vector.tensor_scalar(less[:, :], key_row, key, None, ALU.is_lt))
                settled()
                then(nc.vector.tensor_reduce(counts[:, 1:2], less[:, :], AX.X, ALU.add))
                then(nc.vector.tensor_scalar(facts[:, 4:5], facts[:, 4:5], float(N_LORA0), None, ALU.add))
                settled()
                then(nc.vector.tensor_scalar(one_hot[:, :], num_row[:, :], counts[:, 0:1], counts[:, 1:2],
                                             ALU.subtract, ALU.is_equal))
                assert steps[0] == ORDER_PLACES
                then(nc.vector.tensor_scalar(counts[:, 3:4], counts[:, 0:1], 0.0, None, ALU.is_equal))
                then(nc.vector.tensor_scalar(more[:, :], key_row, key, None, ALU.is_gt))
                assert steps[0] == ORDER_FIRSTS
                dve.wait_ge(order_mm, 2)
                nc.vector.tensor_copy(table[:, T_BATCH:T_LORA],
                                      table_ps[:, T_BATCH:T_LORA]).then_inc(batches_ready, 1)
                dve.wait_ge(order_mm, 3)
                nc.vector.tensor_copy(table[:, T_LORA:T_COND],
                                      table_ps[:, LORA_COL:LORA_COL + 2 * BATCHES]).then_inc(loras_ready, 1)

            def rank_the_matrices():
                settled()
                then(nc.vector.tensor_scalar(counts[:, 1:2], id2, 1.0, counts[:, 3:4], ALU.add, ALU.mult))
                dve.wait_ge(order_mm, 4)
                copy(facts[:, 5:6], sums_ps[0:BATCHES, 0:1])
                settled()
                then(nc.vector.tensor_scalar(rank_hot[:, :], num_row[:, 0:MATS2 + 1], facts[:, 5:6], None, ALU.is_equal))
                assert steps[0] == ORDER_STEPS

            def plan_layer2():
                def slots(first, n=PAIRS):
                    return table[:, T_RANK + first:T_RANK + first + 2 * n].rearrange("o (j s) -> o s j", s=2)[:, 0, :]
                mine, its_second, of_next = slots(0), slots(1, PAIRS), slots(2, PAIRS)
                last = table[:, T_RANK + BATCHES - 1:T_RANK + BATCHES].to_broadcast([1, PAIRS])
                start = table[:, T_START:T_START + PAIRS]
                dve.wait_ge(order_mm, 5)
                nc.vector.tensor_copy(table[:, T_COND:T_FACTS], table_ps[:, T_COND:T_FACTS]).then_inc(table_ready, 1)
                dve.wait_ge(table_ready, 1)
                dve.wait_ge(steps_one, 1)
                nc.vector.tensor_tensor(table[:, T_MIXED:T_MIXED + PAIRS], its_second, mine, ALU.subtract).then_inc(plan_step, 1)
                nc.vector.tensor_tensor(table[:, T_FOLLOWING:T_FOLLOWING + PAIRS], of_next, its_second, ALU.subtract).then_inc(plan_step, 1)
                nc.vector.tensor_tensor(rank_step[:, 1:], slots(2, PAIRS - 1), slots(0, PAIRS - 1), ALU.subtract).then_inc(plan_step, 1)
                nc.vector.tensor_tensor(ranks_left[:, :], last, mine, ALU.subtract).then_inc(plan_step, 1)
                dve.wait_ge(plan_step, 4)
                nc.vector.tensor_tensor(start, rank_step[:, :], ranks_left[:, :], ALU.mult).then_inc(plan_step, 1)
                dve.wait_ge(plan_step, 5)
                nc.vector.tensor_scalar(start, start, 1, None, ALU.min).then_inc(plan_ready, 1)

            def convert(turn, tiles):
                for k in tiles:
                    dve.wait_ge(w_hi, turn * KT + (k + 1))
                    split = w_ring[:, ring_half(turn, k // HK), k % HK]
                    nc.vector.tensor_tensor(split[:, 1, :], w_stage[:, k % STAGES, :], split[:, 0, :],
                                            ALU.subtract).then_inc(w_lo, 1)

            def x_lo(s, p, h, lora):
                dve.wait_ge(x_hi_ready, 2 * s + (h + 1))
                nc.vector.tensor_tensor(xs_of(h, 1), x_of(p, h), xs_of(h, 0), ALU.subtract).then_inc(x_lo_ready, 1)
                if lora:
                    dve.wait_ge(a_hi_ready, 2 * s + (h + 1))
                    for b in range(2):
                        split = a_split_of(h, b)
                        op = nc.vector.tensor_tensor(split[:, :, GROUPS - 1, :], a_of(h, b), split[:, :, 0, :],
                                                     ALU.subtract)
                    op.then_inc(a_lo_ready, 1)

            def low(t, parity):
                dve.wait_ge(quarters, 4 * t + 4)
                dve.wait_ge(y_done, t + 1)
                dve.wait_ge(b_lo, t + 1)
                nc.vector.tensor_tensor(low_a[:, :], low_ps[0:KL, parity, P:2 * P], low_scale[:, :], ALU.mult).then_inc(low_step, 1)
                nc.vector.tensor_tensor(low_sum[:, :], low_ps[0:KL, parity, 0:P], low_scale[:, :], ALU.mult).then_inc(low_step, 1)
                dve.wait_ge(low_step, 4 * t + 2)
                nc.vector.tensor_tensor(low_sum[:, :], low_sum[:, :], low_a[:, :], ALU.add).then_inc(low_step, 1)
                dve.wait_ge(low_step, 4 * t + 3)
                nc.vector.tensor_scalar(low_split[:, :], low_sum[:, :], low_sign[:, 0:1], None, ALU.mult).then_inc(low_step, 1)
                dve.wait_ge(low_step, 4 * t + 4)
                nc.vector.scalar_tensor_tensor(out=low_split[:, :], in0=low_sum[:, :], scalar=low_is_lo[:, 0:1],
                                               in1=low_split[:, :], op0=ALU.mult, op1=ALU.add).then_inc(low_ready, 1)

            def b_lo_part(t):
                dve.wait_ge(b_hi, t + 1)
                nc.vector.scalar_tensor_tensor(out=b_split[:, :], in0=b_stage[:, 0:FEATS], scalar=b_is_lo[:, 0:1],
                                               in1=b_split[:, :], op0=ALU.mult, op1=ALU.add)
                nc.vector.tensor_scalar(low_scale[:, :], low_mask[:, :], b_stage[:, FEATS:FEATS + 1], None,
                                        ALU.mult).then_inc(b_lo, 1)

            def update_x(t, p, layer):
                dve.wait_ge(t_done, t + 3)
                for k in range(KT):
                    x = x_all[:, p, :, k, :]
                    op = nc.vector.scalar_tensor_tensor(
                        out=x, in0=t_ps[:, k * P:(k + 1) * P].rearrange("p (b r) -> p b r", b=2),
                        scalar=bias_sb[:, layer, k:k + 1], in1=x, op0=ALU.add, op1=ALU.add)
                op.then_inc(x_updated, 1)

            def lora_step(t, parity, p, layer, first=False, updated=None, ahead=None, turn=None, lora=True):
                if not first:
                    low(t - 1, 1 - parity)
                    if updated:
                        update_x(t - 2, *updated)
                    b_lo_part(t)
                p_next = p + 1 if turn is None else 0
                x_lo(t + 1, p_next, 0, lora)
                if first:
                    b_lo_part(t)
                if turn is not None:
                    convert(turn, SECOND_HALF)
                x_lo(t + 1, p_next, 1, lora)
                if ahead:
                    convert(*ahead)

            dve.sem_inc(low_ready, 2)
            dve.sem_inc(x_updated, 1)
            dve.sem_inc(out_ready, 1)
            masks()
            order_the_batches()
            convert(0, range(AHEAD))
            x_lo(0, 0, 0, True)
            x_lo(0, 0, 1, True)
            rank_the_matrices()
            convert(0, range(AHEAD, KT))
            dve.wait_ge(bias_in, 16)

            early, late = FIRST_QUARTERS
            lora_step(0, 0, 0, 0, first=True)
            plan_layer2()
            lora_step(1, 1, 1, 0)
            lora_step(2, 0, 2, 0, updated=(0, 0), ahead=(1, early))
            lora_step(3, 1, 3, 0, updated=(1, 0), ahead=(1, late))
            lora_step(4, 0, 4, 0, updated=(2, 0))
            with dve.Fori(2, PAIRS // 2 - 1) as i:
                t = 2 * i + 1
                lora_step(t, 1, t, 0, updated=(t - 2, 0))
                lora_step(t + 1, 0, t + 1, 0, updated=(t - 1, 0))
            lora_step(PAIRS - 1, 1, PAIRS - 1, 0, updated=(PAIRS - 3, 0), turn=1)
            lora_step(PAIRS, 0, 0, 1, updated=(PAIRS - 2, 0))
            lora_step(PAIRS + 1, 1, 1, 1, updated=(PAIRS - 1, 0), ahead=(2, early))
            lora_step(PAIRS + 2, 0, 2, 1, updated=(0, 1), ahead=(2, late))
            with dve.Fori(1, PAIRS // 2 - 1) as i:
                p = 2 * i + 1
                lora_step(p + PAIRS, 1, p, 1, updated=(p - 2, 1))
                lora_step(p + (PAIRS + 1), 0, p + 1, 1, updated=(p - 1, 1))
            dve.wait_ge(plan_ready, 1)
            at_first = (first_rank(dve, 0), *plan(dve, 0))
            lora_step(2 * PAIRS - 1, 1, PAIRS - 1, 1, updated=(PAIRS - 3, 1), turn=2, lora=False)

            def x3_lo_part(j, parity, banks=(slice(0, FEATS),)):
                for n, cols in enumerate(banks):
                    dve.wait_ge(x3_hi_ready, j + 1 + n)
                    nc.vector.tensor_tensor(x3_lo[:, cols], y_ps[:, parity, cols], x3_hi[:, cols],
                                            ALU.subtract).then_inc(y_taken, 1)

            def split_w3(j):
                dve.wait_ge(w3_hi_ready, j + 1)
                nc.vector.tensor_tensor(w3_lo[:, :], w3_stage[:, :], w3_hi[:, :], ALU.subtract).then_inc(w3_lo_ready, 1)

            def switch_step(j, parity, first=False, last=False):
                def rest_of_first_half():
                    with dve.If(start != 0):
                        convert(rank + 3, FIRST_QUARTERS[1])

                if first:
                    rank, mixed, following, start = at_first
                    low(2 * PAIRS - 1, 1)
                    with dve.If(start != 0):
                        convert(rank + 3, FIRST_QUARTERS[0])
                    update_x(2 * PAIRS - 2, PAIRS - 2, 1)
                else:
                    x3_lo_part(j - 1, 1 - parity)
                    rank = first_rank(dve, j)
                    mixed, following, start = plan(dve, j)
                    split_w3(j - 1)
                    with dve.If(start != 0):
                        convert(rank + 3, FIRST_HALF)
                with dve.If(mixed != 0):
                    if first:
                        rest_of_first_half()
                    convert(rank + 3, SECOND_HALF)
                    if not last:
                        with dve.If(following != 0):
                            convert(rank + 4, FIRST_HALF)
                if not last:
                    s = j + (2 * PAIRS + 1)
                    x_lo(s, j + 1, 0, False)
                    if first:
                        with dve.If(mixed == 0):
                            rest_of_first_half()
                    with dve.If(following != 0):
                        convert(rank + mixed + 3, SECOND_HALF)
                    x_lo(s, j + 1, 1, False)

            switch_step(0, 0, first=True)
            update_x(2 * PAIRS - 1, PAIRS - 1, 1)
            with dve.Fori(0, PAIRS // 2 - 1) as i:
                switch_step(2 * i + 1, 1)
                switch_step(2 * i + 2, 0)
            switch_step(PAIRS - 1, 1, last=True)
            split_w3(PAIRS - 1)
            x3_lo_part(PAIRS - 1, 1, BANKS)

        @block.tensor
        def _(pe):
            def slots_of(fact, at, n):
                return nc.tensor.matmul(table_ps[:, at:at + n], facts[:, fact:fact + 1], one_hot[:, 0:n],
                                        start=True, stop=True)

            def order_products():
                pe.wait_ge(iota_ready, 5)
                pe.wait_ge(order_step, ORDER_SAME)
                nc.tensor.matmul(sums_ps[0:BATCHES, 0:BATCHES], ones[:, :], same[:, :], start=True, stop=True)
                nc.tensor.matmul(sums_ps[0:BATCHES, BATCHES:BATCHES + 1], same[:, :], ones[:, 0:1],
                                 start=True, stop=True).then_inc(order_mm, 1)
                pe.wait_ge(order_step, ORDER_PLACES)
                slots_of(0, T_BATCH, SLOTS).then_inc(order_mm, 1)
                slots_of(3, LORA_COL, BATCHES)
                slots_of(4, LORA_COL + BATCHES, BATCHES).then_inc(order_mm, 1)
                pe.wait_ge(order_step, ORDER_FIRSTS)
                nc.tensor.matmul(sums_ps[0:BATCHES, 0:1], more[:, :], counts[:, 3:4],
                                 start=True, stop=True).then_inc(order_mm, 1)

            def rank_products():
                pe.wait_ge(order_step, ORDER_STEPS)
                slots_of(1, T_COND, SLOTS)
                slots_of(5, T_RANK, SLOTS)
                nc.tensor.matmul(table_ps[:, T_USED:T_FACTS], counts[:, 1:2], rank_hot[:, :],
                                 start=True, stop=True).then_inc(order_mm, 1)

            def warm_up():
                for n in range(WARM_UPS):
                    nc.tensor.matmul(y_ps[:, 1, 0:P], ident[:, :], ident[:, :], start=True, stop=True)

            def half(h, parity, half_at, m=P, lora=None, stop=True, first=False, marks=()):
                tiles = range(h * HK, (h + 1) * HK)

                def lora_a(k):
                    if k == tiles[0]:
                        pe.wait_ge(a_hi_ready, 2 * lora + (h + 1))
                        pe.wait_ge(a_lo_ready, 2 * lora + (h + 1))
                    return nc.tensor.matmul(low_ps[0:KL, parity, 0:2 * P], a_split[:, k, :],
                                            xs[:, k].rearrange("p s r -> p (s r)"), start=k == 0, stop=k == KT - 1)

                for k in tiles:
                    if first:
                        pe.wait_ge(w_lo, k + 1)
                    for part_x, part_w in ((0, 0), (0, 1), (1, 0)):
                        if first and k == tiles[0] and part_w == 0:
                            pe.wait_ge((x_hi_ready, x_lo_ready)[part_x], h + 1)
                        for cols in BANKS:
                            op = nc.tensor.matmul(
                                y_ps[0:m, parity, cols], xs[:, k, part_x, 0:m], w_ring[:, half_at, k % HK, part_w, cols],
                                start=k == 0 and part_x == part_w, stop=stop and k == KT - 1 and part_x == 1)
                    if first:
                        if k == tiles[-1]:
                            op = [lora_a(tile) for tile in tiles][-1]
                    elif lora is not None:
                        op = lora_a(k)
                    if k in marks:
                        op.then_inc(quarters, 1)

            def half_by_banks(parity, half_at, m=P):
                for cols in BANKS:
                    for k in SECOND_HALF:
                        for part_x, part_w in ((0, 0), (0, 1), (1, 0)):
                            op = nc.tensor.matmul(
                                y_ps[0:m, parity, cols], xs[:, k, part_x, 0:m], w_ring[:, half_at, k % HK, part_w, cols],
                                start=False, stop=k == KT - 1 and part_x == 1)
                    op.then_inc(quarters, 1)

            def lora_b(t, parity):
                pe.wait_ge(low_ready, t + 3)
                pe.wait_ge(b_lo, t + 1)
                for cols in BANKS:
                    op = nc.tensor.matmul(y_ps[:, parity, cols], low_split[:, :], b_split[:, cols], start=False, stop=True)
                op.then_inc(y_done, 1)

            def transposes(t, parity):
                pe.wait_ge(y_taken, t + 3)
                pe.wait_ge(x_updated, t + 1)
                for k in range(KT):
                    cols = slice(k * P, (k + 1) * P)
                    op = nc.tensor.transpose(t_ps[:, cols], rows[:, parity, cols], ident[:, :])
                op.then_inc(t_done, 1)

            def operands(s, h):
                pe.wait_ge(x_hi_ready, 2 * s + (h + 1))
                pe.wait_ge(x_lo_ready, 2 * s + (h + 1))

            MARKS = (HK - 3, HK - 2, HK - 1, KT - 1)

            def lora_step(t, parity, turn, first=False):
                pe.wait_ge(y_taken, t + 1)
                pe.wait_ge(low_ready, t + 1)
                if not first:
                    operands(t, 0)
                    pe.wait_ge(w_lo, turn * KT + HK)
                half(0, parity, ring_half(turn, 0), lora=t, stop=False, first=first, marks=MARKS)
                if not first:
                    lora_b(t - 1, 1 - parity)
                    operands(t, 1)
                    pe.wait_ge(w_lo, turn * KT + KT)
                half(1, parity, ring_half(turn, 1), lora=t, stop=False, first=first, marks=MARKS)
                if first:
                    rank_products()
                else:
                    transposes(t - 1, 1 - parity)

            pe.sem_inc(y_done, 1)
            pe.sem_inc(t_done, 2)
            pe.sem_inc(l3_done, 1)
            order_products()
            pe.wait_ge(ident_ready, 1)
            warm_up()
            for layer in range(2):
                s = layer * PAIRS
                lora_step(s, 0, layer, first=layer == 0)
                with pe.Fori(0, PAIRS // 2 - 1) as i:
                    lora_step(2 * i + (s + 1), 1, layer)
                    lora_step(2 * i + (s + 2), 0, layer)
                lora_step(s + PAIRS - 1, 1, layer)

            def layer3(j, last=False):
                pe.wait_ge(w3_lo_ready, j + 1)
                pe.wait_ge(x_updated, 2 * PAIRS + 1)
                pe.wait_ge(out_ready, j + 1)
                for n, cols in enumerate(BANKS):
                    pe.wait_ge(y_taken, j + (2 * PAIRS + 3 + (n if last else 0)))
                    for w, x in ((w3_hi, x3_hi), (w3_lo, x3_hi), (w3_hi, x3_lo)):
                        op = nc.tensor.matmul(t_ps[:, cols], w[:, :], x[:, cols],
                                              start=w is w3_hi and x is x3_hi, stop=x is x3_lo)
                    if last or n == NB - 1:
                        op.then_inc(l3_done, 1)

            def switch_step(j, parity, first=False, last=False):
                s = j + 2 * PAIRS
                ra, mixed = first_rank(pe, j), entry(pe, j + T_MIXED, 1)
                rb = ra + 1
                a_half, b_half = (tuple(ring_half(r + 2, h) for h in range(2)) for r in (ra, rb))

                def first_half(marks):
                    pe.wait_ge(y_taken, s + 1)
                    operands(s, 0)
                    pe.wait_ge(w_lo, ra * KT + (2 * KT + HK))
                    half(0, parity, a_half[0], marks=marks)

                def between():
                    if first:
                        lora_b(2 * PAIRS - 1, 1)
                    if last:
                        layer3(j - 1)

                def last_half(at, m=P):
                    if last:
                        half_by_banks(parity, at, m)
                    else:
                        half(1, parity, at, m, marks=(KT - 1,))

                with pe.If(mixed != 0):
                    first_half((HK - 1,))
                    between()
                    operands(s, 1)
                    pe.wait_ge(w_lo, ra * KT + (2 * KT + KT))
                    half(1, parity, a_half[1], marks=(KT - 1,))
                    pe.wait_ge(w_lo, rb * KT + (2 * KT + HK))
                    half(0, parity, b_half[0], m=ROWS, marks=(HK - 1,))
                    pe.wait_ge(w_lo, rb * KT + (2 * KT + KT))
                    last_half(b_half[1], ROWS)
                with pe.Else():
                    first_half(MARKS)
                    between()
                    operands(s, 1)
                    pe.wait_ge(w_lo, ra * KT + (2 * KT + KT))
                    last_half(a_half[1])
                if first:
                    transposes(2 * PAIRS - 1, 1)
                elif not last:
                    layer3(j - 1)

            pe.wait_ge(plan_ready, 1)
            switch_step(0, 0, first=True)
            with pe.Fori(0, PAIRS // 2 - 1) as i:
                switch_step(2 * i + 1, 1)
                switch_step(2 * i + 2, 0)
            switch_step(PAIRS - 1, 1, last=True)
            layer3(PAIRS - 1, last=True)


def kernel(x, itok_B_1_7, itok_B_6_15, itok_B_3_7, itok_B_0_15, L0_cond_weight, L0_cond_bias,
           L0_cond_lora_a_weights, L0_cond_lora_b_weights, L0_cond_scaling_factors, L1_cond_base_weight,
           L1_cond_base_bias, L1_cond_lora_A_w, L1_cond_lora_B_w, L2_cond_weight, L3_cond_weights):
    import numpy as np
    import concourse.bacc as bacc
    from concourse.bass_utils import run_bass_kernel_spmd

    def arr(a):
        return np.asarray(a)

    def a_layout(a):
        n = a.shape[0]
        return arr(a).reshape(n, RANK, KT, P).transpose(0, 3, 2, 1).reshape(n, P, KT * RANK)

    def b_layout(b, scale):
        n = b.shape[0]
        scale = np.broadcast_to(arr(scale)[:, None, None], (n, RANK, 1))
        return np.concatenate([arr(b).transpose(0, 2, 1), scale], axis=2)

    ids = np.stack([arr(i) for i in (itok_B_0_15, itok_B_3_7, itok_B_1_7, itok_B_6_15)], axis=1)
    weights = np.concatenate([arr(L0_cond_weight)[None], arr(L1_cond_base_weight)[None], arr(L2_cond_weight)])
    ones = np.ones(L1_cond_lora_A_w.shape[0], np.float32)
    arrays = {
        "xt": arr(x).reshape(BATCHES, ROWS, KT, P).transpose(0, 3, 2, 1).reshape(BATCHES, P, KT * ROWS),
        "ids_cols": ids.astype(np.int32),
        "ids2_row": arr(itok_B_3_7).reshape(1, BATCHES).astype(np.int32),
        "wt": weights.transpose(0, 2, 1).reshape(2 + MATS2, KT, P, FEATS),
        "bias": np.stack([arr(L0_cond_bias), arr(L1_cond_base_bias)]).reshape(2, KT, P).transpose(2, 0, 1),
        "a_tab": np.concatenate([a_layout(L0_cond_lora_a_weights), a_layout(L1_cond_lora_A_w)]),
        "b_tab": np.concatenate([b_layout(L0_cond_lora_b_weights, L0_cond_scaling_factors),
                                 b_layout(L1_cond_lora_B_w, ones)]),
        "w3": arr(L3_cond_weights),
    }
    arrays = {name: np.ascontiguousarray(a) for name, a in arrays.items()}
    nc = bacc.Bacc("TRN2", target_bir_lowering=False, num_devices=1, dynamic_dma_scratch_size=1024)
    args = {name: nc.dram_tensor(name, a.shape, mybir.dt.from_np(a.dtype), kind="ExternalInput").ap()
            for name, a in arrays.items()}
    out = nc.dram_tensor("out", (BATCHES, ROWS, FEATS), F32, kind="ExternalOutput").ap()
    build(nc, out=out, **args)
    return run_bass_kernel_spmd(nc, [arrays], core_ids=[0]).results[0]["out"]
```
